# Optimizing a Trainium2 kernel written in Bass

```python
import numpy as np
import jax
import jax.numpy as jnp

def _softmax(x, axis=-1):
    return jax.nn.softmax(x, axis=axis)

def _gelu(x):
    return jax.nn.gelu(x, approximate=True)

def _silu(x):
    return jax.nn.silu(x)

def _sigmoid(x):
    return jax.nn.sigmoid(x)

def _layernorm(x, axis=-1, eps=1e-05):
    m = jnp.mean(x, axis=axis, keepdims=True)
    v = jnp.var(x, axis=axis, keepdims=True)
    return (x - m) / jnp.sqrt(v + eps)

def _scatter_add(tgt, idx, src, axis=0):
    return tgt.at[idx].add(src)

def _segment_sum(src, seg, n):
    return jax.ops.segment_sum(src, seg, n)
kernel_name = 'mk_xattn_ffn_d1_seqx_r8_085450'

def setup_inputs(seed: int=0):
    np.random.seed(seed)
    _w = jnp.asarray

    def _rec_inputs():
        import jax
        import jax.numpy as jnp
        _rk = jax.random.key(seed)
        x = 2.818e-05 + 1 * jax.random.normal(jax.random.fold_in(_rk, 1), (4, 256, 256), jnp.float32)
        _lenS = 256 - jax.random.randint(jax.random.fold_in(_rk, 7), (4,), 0, max(1, 256 // 4) + 1, jnp.int32)
        _lenS2 = 256 - jax.random.randint(jax.random.fold_in(_rk, 8), (4,), 0, max(1, 256 // 4) + 1, jnp.int32)
        _ctx_1024P = jax.random.normal(jax.random.fold_in(_rk, 11), (4, 16, 128), jnp.float32)
        _ctx_1024c = jax.random.dirichlet(jax.random.fold_in(_rk, 511), 0.3 * jnp.ones((16,), jnp.float32), (4, 256))
        _ctx_1024t = jnp.einsum('bsk,bkd->bsd', _ctx_1024c, _ctx_1024P)
        _ctx_1024t = _ctx_1024t * jax.lax.rsqrt(jnp.mean(jnp.square(_ctx_1024t)) + 1e-12) * 0.953939
        ctx_1024 = 7.22013e-05 + 1.00017 * (_ctx_1024t + 0.3 * jax.random.normal(jax.random.fold_in(_rk, 611), (4, 256, 128), jnp.float32))
        return (x, ctx_1024)
    x, ctx_1024 = _rec_inputs()

    def _L0_xattn_setup():
        import jax, jax.numpy as jnp
        import numpy as np
        B_, L_, D_MODEL = (4, 256, 128)
        D_STATE, D_CONV, EXPAND = (16, 4, 2)
        D_INNER = EXPAND * D_MODEL
        DT_RANK = (D_MODEL + 15) // 16

        def silu(x):
            return x * jax.nn.sigmoid(x)
        key = jax.random.key(seed)
        ks = jax.random.split(key, 10)
        f32 = jnp.float32
        hidden_states = jax.random.normal(ks[0], (B_, L_, D_MODEL), dtype=f32)
        z = jax.random.normal(ks[1], (B_, D_INNER, L_), dtype=f32)
        in_proj_w = jax.random.normal(ks[2], (D_INNER, D_MODEL), dtype=f32) * 0.02
        conv_w = jax.random.normal(ks[3], (D_INNER, 1, D_CONV), dtype=f32) * 0.1
        conv_b = jax.random.normal(ks[4], (D_INNER,), dtype=f32) * 0.02
        x_proj_w = jax.random.normal(ks[5], (DT_RANK + 2 * D_STATE, D_INNER), dtype=f32) * 0.02
        dt_proj_w = jax.random.uniform(ks[6], (D_INNER, DT_RANK), dtype=f32, minval=-DT_RANK ** (-0.5), maxval=DT_RANK ** (-0.5))
        dt = jnp.exp(jax.random.uniform(ks[7], (D_INNER,), dtype=f32, minval=np.log(0.001), maxval=np.log(0.1)))
        dt_proj_b = jnp.log(jnp.expm1(dt))
        A_log = jnp.log(jnp.broadcast_to(jnp.arange(1, D_STATE + 1, dtype=f32), (D_INNER, D_STATE)))
        D = jnp.ones((D_INNER,), f32)
        return {'hidden_states': hidden_states, 'z': z, 'in_proj_w': in_proj_w, 'conv_w': conv_w, 'conv_b': conv_b, 'x_proj_w': x_proj_w, 'dt_proj_w': dt_proj_w, 'dt_proj_b': dt_proj_b, 'A_log': A_log, 'D': D}
    _L0_xattn_all = _L0_xattn_setup()
    _L0_xattn_in = {k: v for k, v in _L0_xattn_all.items() if k in ('in_proj_w', 'conv_w', 'conv_b', 'x_proj_w', 'dt_proj_w', 'dt_proj_b', 'A_log', 'D')}
    del _L0_xattn_all

    def _L0_ffn_setup():
        import jax, jax.numpy as jnp
        import numpy as np
        B, S, H, E, I, K = (2, 64, 256, 64, 128, 8)
        key = jax.random.key(seed)
        k0, k1, k2, k3, k4 = jax.random.split(key, 5)
        return {'hidden_states': jax.random.normal(k0, (B, S, H), jnp.float32), 'router_w': jax.random.normal(k1, (E, H), jnp.float32) * 0.02, 'w_gate': jax.random.normal(k2, (E, I, H), jnp.float32) * 0.02, 'w_up': jax.random.normal(k3, (E, I, H), jnp.float32) * 0.02, 'w_down': jax.random.normal(k4, (E, H, I), jnp.float32) * 0.02}
    _L0_ffn_all = _L0_ffn_setup()
    _L0_ffn_in = {k: v for k, v in _L0_ffn_all.items() if k in ('router_w', 'w_gate', 'w_up', 'w_down')}
    del _L0_ffn_all
    return {'x': x, 'ctx_1024': ctx_1024, 'L0_xattn_in_proj_w': _L0_xattn_in['in_proj_w'], 'L0_xattn_conv_w': _L0_xattn_in['conv_w'], 'L0_xattn_conv_b': _L0_xattn_in['conv_b'], 'L0_xattn_x_proj_w': _L0_xattn_in['x_proj_w'], 'L0_xattn_dt_proj_w': _L0_xattn_in['dt_proj_w'], 'L0_xattn_dt_proj_b': _L0_xattn_in['dt_proj_b'], 'L0_xattn_A_log': _L0_xattn_in['A_log'], 'L0_xattn_D': _L0_xattn_in['D'], 'L0_ffn_router_w': _L0_ffn_in['router_w'], 'L0_ffn_w_gate': _L0_ffn_in['w_gate'], 'L0_ffn_w_up': _L0_ffn_in['w_up'], 'L0_ffn_w_down': _L0_ffn_in['w_down']}

def reference(x, ctx_1024, L0_xattn_in_proj_w, L0_xattn_conv_w, L0_xattn_conv_b, L0_xattn_x_proj_w, L0_xattn_dt_proj_w, L0_xattn_dt_proj_b, L0_xattn_A_log, L0_xattn_D, L0_ffn_router_w, L0_ffn_w_gate, L0_ffn_w_up, L0_ffn_w_down):
    import jax
    import jax.numpy as jnp

    def _L0_xattn_ref(hidden_states, z, in_proj_w, conv_w, conv_b, x_proj_w, dt_proj_w, dt_proj_b, A_log, D):
        import jax, jax.numpy as jnp
        import numpy as np
        B_, L_, D_MODEL = (4, 256, 128)
        D_STATE, D_CONV, EXPAND = (16, 4, 2)
        D_INNER = EXPAND * D_MODEL
        DT_RANK = (D_MODEL + 15) // 16

        def silu(x):
            return x * jax.nn.sigmoid(x)
        Bsz, L, _ = hidden_states.shape
        d_inner, _, d_conv = conv_w.shape
        dt_rank = dt_proj_w.shape[1]
        d_state = A_log.shape[1]
        x = jnp.einsum('bld,ed->bel', hidden_states, in_proj_w)
        xc = jax.lax.conv_general_dilated(x, conv_w, window_strides=(1,), padding=[(d_conv - 1, 0)], feature_group_count=d_inner, dimension_numbers=('NCH', 'OIH', 'NCH'))
        x = silu(xc + conv_b[None, :, None])
        x_dbl = jnp.einsum('bdl,ed->bel', x, x_proj_w)
        dt_low, Bm, Cm = jnp.split(x_dbl, [dt_rank, dt_rank + d_state], axis=1)
        dt = jnp.einsum('brl,dr->bdl', dt_low, dt_proj_w)
        dt = jax.nn.softplus(dt + dt_proj_b[None, :, None])
        A = -jnp.exp(A_log)
        dt_t = jnp.moveaxis(dt, -1, 0)
        B_t = jnp.moveaxis(Bm, -1, 0)
        C_t = jnp.moveaxis(Cm, -1, 0)
        u_t = jnp.moveaxis(x, -1, 0)

        def step(state, inp):
            d, b, c, u = inp
            dA = jnp.exp(d[..., None] * A)
            state = state * dA + (d * u)[..., None] * b[:, None, :]
            y = jnp.einsum('bdn,bn->bd', state, c)
            return (state, y)
        state0 = jnp.zeros((Bsz, d_inner, d_state), x.dtype)
        _, ys = jax.lax.scan(step, state0, (dt_t, B_t, C_t, u_t))
        y = jnp.moveaxis(ys, 0, 2)
        y = y + D[None, :, None] * x
        y = y * silu(z)
        return jnp.swapaxes(y, 1, 2)

    def _L0_ffn_ref(hidden_states, router_w, w_gate, w_up, w_down):
        import jax, jax.numpy as jnp
        import numpy as np
        B, S, H, E, I, K = (2, 64, 256, 64, 128, 8)
        b, s, h = hidden_states.shape
        x = hidden_states.reshape(-1, h)
        T = x.shape[0]
        logits = x @ router_w.T
        probs = jax.nn.softmax(logits.astype(jnp.float32), axis=-1)
        top_w, top_i = jax.lax.top_k(probs, K)
        top_w = top_w.astype(x.dtype)
        combine = jnp.zeros((T, E), x.dtype).at[jnp.arange(T)[:, None], top_i].add(top_w)
        g = jnp.einsum('th,eih->tei', x, w_gate)
        u = jnp.einsum('th,eih->tei', x, w_up)
        hmid = jax.nn.silu(g) * u * combine[:, :, None]
        out = jnp.einsum('tei,ehi->th', hmid, w_down)
        return out.reshape(b, s, h)
    x = x + _L0_xattn_ref(ctx_1024, _layernorm(x, axis=-1), L0_xattn_in_proj_w, L0_xattn_conv_w, L0_xattn_conv_b, L0_xattn_x_proj_w, L0_xattn_dt_proj_w, L0_xattn_dt_proj_b, L0_xattn_A_log, L0_xattn_D)
    x = x + _L0_ffn_ref(_layernorm(x, axis=-1), L0_ffn_router_w, L0_ffn_w_gate, L0_ffn_w_up, L0_ffn_w_down)
    return x

_drawn_inputs = setup_inputs


def setup_inputs(seed=0):
    import zlib

    import numpy as np

    out = dict(_drawn_inputs(seed))
    spreads = {'L0_xattn_D': (1.0, 0.2)}
    factors = {}
    for name, (base, spread) in spreads.items():
        noise = np.random.default_rng([zlib.crc32(name.encode()), seed]).standard_normal(out[name].shape)
        drawn = base * np.exp(spread * noise) if base else spread * noise
        out[name] = jnp.asarray(drawn.astype(out[name].dtype))
    for name, factor in factors.items():
        out[name] = (out[name] * factor).astype(out[name].dtype)
    return out
```

```python
from contextlib import ExitStack

import numpy as np
import concourse.bass as bass
from concourse import mybir

F32 = mybir.dt.float32
BF16 = mybir.dt.bfloat16
U32 = mybir.dt.uint32
U16 = mybir.dt.uint16
ALU = mybir.AluOpType
ACT = mybir.ActivationFunctionType
AX_X = mybir.AxisListType.X

P = 128
NB, L, DM, DI = 4, 256, 128, 256
H = 256
NS, KC, R = 16, 4, 8
E, TOPK, I = 64, 8, 128
C2 = DI // P
T = NB * L
NT = T // P
HN = NS // 2
STEPS = NB * C2 * 2
SPB = C2 * 2

LN_EPS = 1e-5

C_GROUPS = (0, 1, 3, 6, NS // 2)

CONV_BANK = (4, 7, 6, 5)
XDBL_BANK = (6, 7, 6, 5)

CAP = 192
HALF = CAP // 2
ROW = H + E + 1
SLOTS = E * CAP
OVER = SLOTS + E * T
KEY = 1 << 17
SPARE = T
WROW = 2 * C2 * I + H
RING = 8


def pool_states(s):
    return 6 if s < SPB + 2 else 4


def consts():
    one = 0x3F80
    sel = np.zeros((96, 2 * NS, P), np.uint16)
    for j in range(2 * NS):
        for part in range(3):
            sel[32 * part + j, j, :] = one
    ones = np.full((P, P), one, np.uint16)
    tri = np.triu(ones, 1)
    e = np.arange(E)
    over = np.broadcast_to((SLOTS + (T - CAP) * e).astype(np.float32), (P, C2, E))
    base = np.broadcast_to((KEY - CAP * e).astype(np.float32), (P, C2, E))
    return {
        "c_sel": sel.reshape(96, -1),
        "c_tri": np.concatenate([tri, ones], 1),
        "c_ident": np.eye(P, dtype=np.float32),
        "c_place": np.ascontiguousarray(np.stack([over, base], 1).reshape(P, -1)),
    }


def program(nc, d, out):
    with ExitStack() as ctx:
        def sb(name, shape, dt=F32):
            return ctx.enter_context(nc.sbuf_tensor(name, shape, dt))

        def sem(name):
            return ctx.enter_context(nc.semaphore(name))

        ps = ctx.enter_context(nc.psum_tensor("ps", [P, 8, 512], F32))
        ps_b = [ps[:, 2 * q:2 * q + 2, :].rearrange("p a f -> p (a f)") for q in range(2)]
        ps_c, ps_y, ps_prep, ps_post = (ps[:, k, :] for k in (4, 5, 6, 7))

        def c_bank(b, g):
            return ps_prep if b >= 1 and g % 2 else ps_c

        slots = nc.dram_tensor("slots", (OVER, ROW), F32, kind="Internal").ap()
        sums = [nc.dram_tensor(f"sums{q}", (T + CAP, H), F32, kind="Internal").ap() for q in range(2)]

        sel = sb("sel", [96, 2 * NS, P], BF16)
        tri = sb("tri", [P, 2, P], BF16)
        ident = sb("ident", [P, P])
        place = sb("place", [P, 2, C2 * E])
        ctx_pad = sb("ctx_pad", [P, NB, L + KC - 1])
        in_proj = sb("in_proj", [P, C2, DM])
        vecs = sb("vecs", [P, C2, KC + 3 + NS])
        xp_w = sb("xp_w", [P, C2, 104])
        dt_w = sb("dt_w", [104, DI])
        rt_w = sb("rt_w", [P, C2, E])
        scaled = sb("scaled", [P, C2, KC, DM])
        conv_w = sb("conv_w", [P, C2, KC, P])
        a_exp = sb("a_exp", [P, C2, NS])
        a_neg = sb("a_neg", [P, C2, NS])
        x_sb = sb("x_sb", [P, NT, H])
        x2 = sb("x2", [P, NT, H])
        rows = sb("rows", [P, NT, ROW])
        hT = sb("hT", [P, C2, L])
        fill = sb("fill", [HALF, 2, ROW])
        u = sb("u", [P, NB, C2, L])
        bc = sb("bc", [96, NB, L], BF16)
        bc_rest = sb("bc_rest", [96, L])
        dt_low = sb("dt_low", [104, NB, L])
        dt_pos = sb("dt_pos", [P, C2, L])
        dt_abs = sb("dt_abs", [P, C2, L])
        dt_e = sb("dt_e", [P, C2, L])
        dt_ln = sb("dt_ln", [P, C2, L])
        dt_t = sb("dt_t", [P, C2, L])
        dt = sb("dt", [P, 2, C2, L])
        du = sb("du", [P, 2, C2, L])
        dA = sb("dA", [P, 2, HN, L])
        dBu = sb("dBu", [P, HN, L])
        hs = sb("hs", [P, 2, HN, L])
        c_sb = sb("c_sb", [P, 2, NS, L])
        st = sb("st", [P, NT, 6])
        mv = sb("mv", [P, NT, 2])
        var = sb("var", [P, NT, 1])
        rstd = sb("rstd", [P, NT, 1])
        newton = sb("newton", [P, NT, 1])
        nmr = sb("nmr", [P, NT, 1])
        gz = sb("gz", [P, NB, C2, L])
        yg = sb("yg", [P, C2, L])
        st2 = sb("st2", [P, C2, 6])
        mv2 = sb("mv2", [P, C2, 2])
        rstd2 = sb("rstd2", [P, C2, 1])
        nmr2 = sb("nmr2", [P, C2, 1])
        var2 = sb("var2", [P, C2, 1])
        newton2 = sb("newton2", [P, C2, 1])
        neg_max = sb("neg_max", [P, C2])
        ex = sb("ex", [P, C2, E])
        ex_sum = sb("ex_sum", [P, C2])
        inv_sum = sb("inv_sum", [P, C2])
        top = sb("top", [P, C2, TOPK])
        rest = sb("rest", [P, C2, E])
        mask = sb("mask", [P, C2, E], BF16)
        seen = sb("seen", [P, E], BF16)
        r_over = sb("r_over", [P, C2 * E])
        r_key = sb("r_key", [P, C2 * E])
        key_top = sb("key_top", [P, C2, TOPK])
        slot_of = sb("slot_of", [P, NT, TOPK], U32)
        count = sb("count", [P, 1])
        flag = sb("flag", [P, 1], U32)
        tick = sb("tick", [P, 2])
        w_ring = sb("w_ring", [P, RING, WROW])
        xs = c_sb[0:HALF].rearrange("p a n l -> p (a n l)")[:, 0:RING * 2 * ROW].rearrange(
            "p (i j f) -> p i j f", i=RING, j=2)
        xT = sb("xT", [P, 2, C2, CAP])
        w_slot = sb("w_slot", [HALF, RING, 2])
        sg = sb("sg", [P, 2, CAP])
        mid = sb("mid", [P, 2, CAP])
        y_sb = hs[0:HALF].rearrange("p a n l -> p (a n l)").rearrange("p (i j h) -> p i j h", i=RING, j=2)
        TH = T // 2
        hT_all = c_sb[:].rearrange("p a n l -> p (a n l)")[:, 0:C2 * T].rearrange("p (c t) -> p c t", c=C2)
        sg_all = c_sb[:].rearrange("p a n l -> p (a n l)")[:, C2 * T:C2 * T + T].rearrange("p (q t) -> p q t", q=2)
        mid_all = c_sb[:].rearrange("p a n l -> p (a n l)")[:, C2 * T + T:C2 * T + 2 * T].rearrange(
            "p (q t) -> p q t", q=2)
        w_tok = sb("w_tok", [P, 2, NT])
        back = [dA[:, q].rearrange("p n l -> p (n l)").rearrange("p (s t h) -> p s t h", s=2, h=H)
                for q in range(2)]

        s_ctx, s_small, s_const, s_x = (sem(n) for n in ("s_ctx", "s_small", "s_const", "s_x"))
        s_router = sem("s_router")
        fill_made, fill_done = sem("fill_made"), sem("fill_done")
        id_made = sem("id_made")
        edges = sem("edges")
        dve_seq = sem("dve_seq")
        scaled_ready, taps_ready, conv_w_ready = sem("scaled_ready"), sem("taps_ready"), sem("conv_w_ready")
        act_seq, a_ready, s_ident = sem("act_seq"), sem("a_ready"), sem("s_ident")
        xc_ready, u_ready = sem("xc_ready"), sem("u_ready")
        xdbl_ready, low_ready, bc_ready, dtv_ready = (
            sem(n) for n in ("xdbl_ready", "low_ready", "bc_ready", "dtv_ready"))
        act_soft, soft_used, soft_ready, pool_seq, dt_ready = (
            sem(n) for n in ("act_soft", "soft_used", "soft_ready", "pool_seq", "dt_ready"))
        dA_ready, scan_done = sem("dA_ready"), sem("scan_done")
        b_ready, b_used, c_ready, c_copied = sem("b_ready"), sem("b_used"), sem("c_ready"), sem("c_copied")
        hc_pool, hc_dve, y_added = sem("hc_pool"), sem("hc_dve"), sem("y_added")
        z_stats, gz_ready = sem("z_stats"), sem("gz_ready")
        e1_ready = sem("e1_ready")
        z_var, z_root, x2_var, x2_root = (
            sem(n) for n in ("z_var", "z_root", "x2_var", "x2_root"))
        yg_ready, yT_ready, h_ready, hT_psum, hT_ready, logits_ready = (
            sem(n) for n in ("yg_ready", "yT_ready", "h_ready", "hT_psum", "hT_ready", "logits_ready"))
        max_ready, ex_ready, mask_ready, rank_ready, rank_used, place_ready = (
            sem(n) for n in ("max_ready", "ex_ready", "mask_ready", "rank_ready", "rank_used", "place_ready"))
        ticked = sem("ticked")
        weights_ready = sem("weights_ready")
        sent = sem("sent")
        count_ready, flag_ready = sem("count_ready"), sem("flag_ready")
        w_loaded = [sem(f"w_loaded{i}") for i in range(RING)]
        xs_loaded = [sem(f"xs_loaded{i}") for i in range(RING)]
        added = [sem(f"added{i}") for i in range(RING)]
        xT_psum, xT_ready, gu_ready, sg_ready, mid_ready, y_ready, y_scaled, ws_ready = (
            sem(n) for n in ("xT_psum", "xT_ready", "gu_ready", "sg_ready", "mid_ready", "y_ready", "y_scaled", "ws_ready"))
        s_back, total_ready, s_out = [sem(f"s_back{i}") for i in range(2)], sem("total_ready"), sem("s_out")
        dn_w = [sem(f"dn_w{i}") for i in range(2)]
        dn_tp, dn_t, dn_wt, dn_g, dn_s, dn_m, dn_y, dn_acc = (
            sem(n) for n in ("dn_tp", "dn_t", "dn_wt", "dn_g", "dn_s", "dn_m", "dn_y", "dn_acc"))

        CB, DTB, DD, AL = KC, KC + 1, KC + 2, KC + 3
        expert_w = d["w_all"]
        slot_view = slots[0:SLOTS, :].rearrange("(e p j) f -> e p j f", p=HALF, j=2)
        out_rows = out.rearrange("b l h -> (b l) h").rearrange("(t p) h -> p t h", p=P)
        x_rows = d["x"].rearrange("b l h -> (b l) h").rearrange("(t p) h -> p t h", p=P)

        def step_of(s):
            return s // SPB, (s // 2) % C2, s % 2

        block = ctx.enter_context(nc.Block())

        @block.sync
        def _(sp):
            for name, tile in (("in_proj", in_proj), ("vecs", vecs)):
                sp.dma_start(tile[:], d[name]).then_inc(s_small, 16)
            sp.dma_start(ctx_pad[:], d["ctxT"]).then_inc(s_ctx, 16)
            sp.dma_start(ident[:], d["c_ident"]).then_inc(s_ident, 16)
            sp.dma_start(xp_w[:], d["xp_w"]).then_inc(s_const, 16)
            sp.dma_start(dt_w[96:104, :], d["dt_wT"]).then_inc(s_const, 16)
            sp.dma_start(sel[:].bitcast(U16), d["c_sel"].rearrange("k (j m) -> k j m", m=P)).then_inc(s_const, 16)
            sp.dma_start(x_sb[:], x_rows).then_inc(s_x, 16)
            sp.dma_start(rt_w[:], d["rt_w"]).then_inc(s_router, 16)
            sp.dma_start(tri[:].bitcast(U16), d["c_tri"].rearrange("p (a m) -> p a m", a=2)).then_inc(s_router, 16)
            sp.dma_start(place[:], d["c_place"].rearrange("p (a m) -> p a m", a=2)).then_inc(s_router, 16)
            sp.wait_ge(fill_made, 2)
            for q in range(4):
                n = E // 4
                src = fill[:].rearrange("p j f -> p (j f)").unsqueeze(1).to_broadcast([HALF, n, 2 * ROW])
                sp.dma_start(slot_view[q * n:(q + 1) * n].rearrange("e p j f -> p e (j f)"),
                             src).then_inc(fill_done, 16)
            for s in range(2):
                sp.dma_start(sums[s].rearrange("(r p) h -> p r h", p=64),
                             fill[0:64, 0, 0:H].unsqueeze(1).to_broadcast([64, (T + CAP) // 64, H]),
                             ).then_inc(fill_done, 16)
            for i in range(RING):
                sp.dma_start(w_ring[:, i, :], expert_w[i]).then_inc(w_loaded[i], 16)

            sp.wait_ge(flag_ready, 1)
            overflow = sp.value_load(flag[0:1, 0:1], min_val=0, max_val=1)
            with sp.If(overflow):
                for i in range(RING):
                    sp.wait_ge(w_loaded[i], 16)

                def load_dense(e, i):
                    if not isinstance(e, int):
                        sp.wait_ge(dn_y, 2 * e - 2)
                    sp.dma_start(w_ring[:, i, :], expert_w[bass.ds(e, 1)].rearrange("e p w -> (e p) w")
                                 ).then_inc(dn_w[i], 16)

                for i in range(2):
                    load_dense(i, i)
                with sp.Fori(1, E // 2) as g:
                    for i in range(2):
                        load_dense(2 * g + i, i)
                sp.wait_ge(dn_acc, 2 * E)
                sp.dma_start(out_rows, x2[:]).then_inc(s_out, 16)
                sp.wait_ge(s_out, 16)
            with sp.Else():
                sp.wait_ge(sent, 16 * NT * TOPK)

                def load(e, i, g):
                    if g is not None:
                        sp.wait_ge(y_ready, e - RING + 1)
                        sp.dma_start(w_ring[:, i, :], expert_w[bass.ds(e, 1)].rearrange("e p w -> (e p) w")
                                     ).then_inc(w_loaded[i], 16)
                        sp.wait_ge(added[i], 32 * g)
                    src = slot_view[bass.ds(e, 1)] if g is not None else slot_view[e:e + 1]
                    sp.dma_start(xs[:, i, :, :], src.rearrange("e p j f -> (e p) j f")).then_inc(xs_loaded[i], 16)

                for i in range(RING):
                    load(i, i, None)
                with sp.Fori(1, E // RING) as g:
                    for i in range(RING):
                        load(g * RING + i, i, g)
                for i in range(RING):
                    sp.wait_ge(added[i], 32 * (E // RING))
                for q in range(2):
                    for s in range(2):
                        src = sums[s][q * (T // 2):(q + 1) * (T // 2), :].rearrange("(t p) h -> p t h", p=P)
                        sp.dma_start(back[q][:, s], src).then_inc(s_back[q], 16)
                for q in range(2):
                    sp.wait_ge(total_ready, q + 1)
                    sp.dma_start(out_rows[:, q * (NT // 2):(q + 1) * (NT // 2), :],
                                 x2[:, q * (NT // 2):(q + 1) * (NT // 2), :]).then_inc(s_out, 16)
                sp.wait_ge(s_out, 32)

        @block.tensor
        def _(pe):
            def bank_of(b):
                return ps[:, CONV_BANK[b], :]

            def prep_x(b, c):
                if b == 2 and c == 0:
                    pe.wait_ge(bc_ready, 1)
                    pe.wait_ge(low_ready, 1)
                for k in range(KC):
                    mm = pe.matmul(bank_of(b)[:, c * L:(c + 1) * L], conv_w[:, c, k, :],
                                   ctx_pad[:, b, k:k + L], start=(k == 0), stop=(k == KC - 1))
                mm.then_inc(xc_ready, 1)

            def prep_bc(b):
                pe.wait_ge(u_ready, b + 1)
                if b == 0:
                    pe.wait_ge(s_const, 16 * 3)
                o = ps[0:104, XDBL_BANK[b], 0:L]
                for c in range(C2):
                    mm = pe.matmul(o, xp_w[:, c, :], u[:, b, c, :], start=(c == 0), stop=(c == C2 - 1))
                mm.then_inc(xdbl_ready, 1)

            def prep_dt(b):
                if b == 0:
                    pe.wait_ge(low_ready, 1)
                elif b == 1:
                    pe.wait_ge(low_ready, 3)
                    pe.wait_ge(bc_ready, 3)
                else:
                    pe.wait_ge(c_copied, b * HN)
                o = ps[:, 0, :] if b == 0 else ps_prep
                for c in range(C2):
                    mm = pe.matmul(o[:, c * L:(c + 1) * L], dt_w[96:96 + R, c * P:(c + 1) * P],
                                   dt_low[96:96 + R, b, :], start=True, stop=True)
                mm.then_inc(dtv_ready, 1)

            def spread_b(s, q):
                b, c, h = step_of(s)
                pe.wait_ge(bc_ready, b + 1)
                if s >= 1:
                    pe.wait_ge(b_used, 2 * (s - 1) + q + 1)
                elif q == 0:
                    pe.wait_ge(soft_used, 1)
                for k in range(4):
                    mm = pe.matmul(ps_b[q][:, k * L:(k + 1) * L], sel[:, h * HN + 4 * q + k, :],
                                   bc[:, b, :], start=True, stop=True)
                mm.then_inc(b_ready, 1)

            def spread_c(b, n0, n1):
                for g in range(n0, n1):
                    pe.wait_ge(bc_ready, b + 1)
                    if b == 0 and g >= 1:
                        pe.wait_ge(c_copied, g)
                    elif b >= 1:
                        pe.wait_ge(c_copied, b * HN + max(g - 1, 0))
                        if g == 1:
                            pe.wait_ge(soft_used, b + 1)
                    for k in range(2):
                        mm = pe.matmul(c_bank(b, g)[:, k * L:(k + 1) * L], sel[:, NS + 2 * g + k, :],
                                       bc[:, b, :], start=True, stop=True)
                    mm.then_inc(c_ready, 1)

            def add_states(s, half):
                b, c, h = step_of(s)
                if half == 0:
                    if s == 0:
                        pe.wait_ge(bc_ready, 4)
                        pe.wait_ge(low_ready, 4)
                    if c == 0 and h == 0 and b >= 1:
                        pe.wait_ge(yg_ready, b)
                    pe.wait_ge(hc_pool, s + 1)
                    pe.wait_ge(hc_dve, s + 1)
                for n in range(half * HN // 2, (half + 1) * HN // 2):
                    mm = pe.matmul(ps_y[:, c * L:(c + 1) * L], ident[:], hs[:, s % 2, n, :],
                                   start=(h == 0 and n == 0), stop=(h == 1 and n == HN - 1))
                if half == 1:
                    mm.then_inc(y_added, 1)

            def turn_y(b):
                pe.wait_ge(yg_ready, b + 1)
                if b >= 1:
                    pe.wait_ge(rank_used, b)
                else:
                    pe.wait_ge(low_ready, 2)
                    pe.wait_ge(bc_ready, 2)
                for c in range(C2):
                    for lc in range(C2):
                        mm = pe.transpose(ps_post[:, lc * H + c * P:lc * H + (c + 1) * P],
                                          yg[:, c, lc * P:(lc + 1) * P], ident[:])
                mm.then_inc(yT_ready, 1)

            def turn_h(b):
                pe.wait_ge(h_ready, b + 1)
                for lc in range(C2):
                    for c in range(C2):
                        mm = pe.transpose(ps_post[:, c * L + lc * P:c * L + (lc + 1) * P],
                                          rows[:, 2 * b + lc, c * P:(c + 1) * P], ident[:])
                mm.then_inc(hT_psum, 1)

            def router(b):
                pe.wait_ge(hT_ready, b + 1)
                if b == 0:
                    pe.wait_ge(s_router, 16 * 3)
                for lc in range(C2):
                    for c in range(C2):
                        mm = pe.matmul(ps_post[:, lc * E:(lc + 1) * E],
                                       hT[:, c, lc * P:(lc + 1) * P], rt_w[:, c, :],
                                       start=(c == 0), stop=(c == C2 - 1))
                mm.then_inc(logits_ready, 1)

            def ranks(b):
                pe.wait_ge(mask_ready, b + 1)
                strict, ones = tri[:, 0, :], tri[:, 1, :]
                for lc in range(C2):
                    o = ps_post[:, 256 + lc * E:256 + (lc + 1) * E]
                    pe.matmul(o, strict, mask[:, lc, :], start=True, stop=False)
                    mm = pe.matmul(o, ones, seen[:], start=False, stop=(lc == 0))
                    if lc:
                        mm = pe.matmul(o, ones, mask[:, 0, :], start=False, stop=True)
                mm.then_inc(rank_ready, 1)

            pe.wait_ge(scaled_ready, 2)
            pe.wait_ge(s_ident, 16)
            for c in range(C2):
                for k in range(KC):
                    mm = pe.transpose(ps[:, 6 + c, k * P:(k + 1) * P], scaled[:, c, k, :], ident[:])
                mm.then_inc(taps_ready, 1)
            pe.wait_ge(conv_w_ready, 2)
            pe.wait_ge(s_ctx, 16)
            for c in range(C2):
                prep_x(0, c)
            prep_bc(0)
            prep_dt(0)
            spread_b(0, 0)
            spread_b(0, 1)
            pe.wait_ge(u_ready, 1)
            for b in range(1, NB):
                for c in range(C2):
                    spread_c(0, 2 * b + c - 2, 2 * b + c - 1)
                    prep_x(b, c)
            spread_c(0, 6, 8)
            for b in range(1, NB):
                prep_bc(b)
            for s in range(STEPS):
                b, c, h = step_of(s)
                k = s % SPB
                if b >= 1 and k == 1:
                    turn_y(b - 1)
                if b >= 1 and k == 2:
                    turn_h(b - 1)
                if s >= 1:
                    add_states(s - 1, 0)
                if s + 1 < STEPS:
                    spread_b(s + 1, 0)
                if s >= 1:
                    add_states(s - 1, 1)
                if s + 1 < STEPS:
                    spread_b(s + 1, 1)
                if k == 0 and b + 1 < NB:
                    prep_dt(b + 1)
                if b >= 1 and k == 2:
                    router(b - 1)
                if b >= 1 and k == 3:
                    ranks(b - 1)
                if b + 1 < NB:
                    spread_c(b + 1, C_GROUPS[k], C_GROUPS[k + 1])
            for half in range(2):
                add_states(STEPS - 1, half)
            turn_y(NB - 1)
            turn_h(NB - 1)
            router(NB - 1)
            ranks(NB - 1)
            pe.wait_ge(place_ready, NB)
            pe.matmul(ps_post[:, 0:E], tri[:, 1, :], seen[:], start=True, stop=True).then_inc(count_ready, 1)

            def turn(e, i, g):
                pe.wait_ge(xs_loaded[i], 16 * (g + 1))
                if not (isinstance(e, int) and e < 2):
                    pe.wait_ge(xT_ready, e - 1)
                for j in range(2):
                    for c in range(C2):
                        mm = pe.transpose(ps[:, i % 2, c * CAP + j * HALF:c * CAP + (j + 1) * HALF],
                                          xs[:, i, j, c * P:(c + 1) * P], ident[0:HALF, 0:HALF])
                mm.then_inc(xT_psum, 1)

            def gate_up(e, i, g):
                pe.wait_ge(w_loaded[i], 16 * (g + 1))
                pe.wait_ge(xT_ready, e + 1)
                if not (isinstance(e, int) and e < 2):
                    pe.wait_ge(mid_ready, e - 1)
                for m in range(2):
                    for c in range(C2):
                        w = w_ring[:, i, (m * C2 + c) * I:(m * C2 + c + 1) * I]
                        mm = pe.matmul(ps[:, 2 + i % 2, m * 256:m * 256 + CAP], w, xT[:, i % 2, c, :],
                                       start=(c == 0), stop=(c == C2 - 1))
                mm.then_inc(gu_ready, 1)

            def down(e, i, g):
                pe.wait_ge(mid_ready, e + 1)
                if not (isinstance(e, int) and e < 2):
                    pe.wait_ge(y_scaled, e - 1)
                for j in range(2):
                    mm = pe.matmul(ps[0:HALF, 4 + i % 2, j * H:(j + 1) * H],
                                   mid[:, i % 2, j * HALF:(j + 1) * HALF], w_ring[:, i, 2 * C2 * I:WROW],
                                   start=True, stop=True)
                mm.then_inc(y_ready, 1)

            pe.wait_ge(flag_ready, 1)
            overflow = pe.value_load(flag[0:1, 0:1], min_val=0, max_val=1)
            with pe.If(overflow):
                for t in range(NT):
                    if t >= 2:
                        pe.wait_ge(dn_t, t - 1)
                    for c in range(C2):
                        mm = pe.transpose(ps[:, t % 2, c * P:(c + 1) * P], rows[:, t, c * P:(c + 1) * P], ident[:])
                    mm.then_inc(dn_tp, 1)
                pe.wait_ge(dn_t, NT)

                def dense_expert(e, i, g):
                    pe.wait_ge(dn_w[i], 16 * (g + 1))
                    for q in range(2):
                        if not (isinstance(e, int) and e == 0):
                            pe.wait_ge(dn_m, 2 * e + q - 1)
                        for m in range(2):
                            for c in range(C2):
                                w = w_ring[:, i, (m * C2 + c) * I:(m * C2 + c + 1) * I]
                                mm = pe.matmul(ps[:, 2 * q + m, :], w, hT_all[:, c, q * TH:(q + 1) * TH],
                                               start=(c == 0), stop=(c == C2 - 1))
                        mm.then_inc(dn_g, 1)
                    for q in range(2):
                        pe.wait_ge(dn_m, 2 * e + q + 1)
                        if not (isinstance(e, int) and e == 0):
                            pe.wait_ge(dn_acc, 2 * e + q - 1)
                        for t in range(NT // 2):
                            mm = pe.matmul(ps[:, 4 + 2 * q + t // 2, t % 2 * H:(t % 2 + 1) * H],
                                           mid_all[:, q, t * P:(t + 1) * P], w_ring[:, i, 2 * C2 * I:WROW],
                                           start=True, stop=True)
                        mm.then_inc(dn_y, 1)

                for i in range(2):
                    dense_expert(i, i, 0)
                with pe.Fori(1, E // 2) as g:
                    for i in range(2):
                        dense_expert(2 * g + i, i, g)
            with pe.Else():
                for e in range(RING):
                    turn(e, e, 0)
                    if e >= 1:
                        gate_up(e - 1, e - 1, 0)
                    if e >= 2:
                        down(e - 2, e - 2, 0)
                with pe.Fori(1, E // RING) as g:
                    for i in range(RING):
                        e = g * RING + i
                        turn(e, i, g)
                        gate_up(e - 1, (i - 1) % RING, g if i >= 1 else g - 1)
                        down(e - 2, (i - 2) % RING, g if i >= 2 else g - 1)
                gate_up(E - 1, RING - 1, E // RING - 1)
                down(E - 2, RING - 2, E // RING - 1)
                down(E - 1, RING - 1, E // RING - 1)

        @block.scalar
        def _(act):
            def copy_c(b, n0, n1):
                for g in range(n0, n1):
                    if g == 0 and b >= 2:
                        act.wait_ge(hc_pool, SPB * (b - 1))
                        act.wait_ge(hc_dve, SPB * (b - 1))
                    act.wait_ge(c_ready, b * HN + g + 1)
                    act.activation(c_sb[:, b % 2, 2 * g:2 * g + 2, :].rearrange("p n l -> p (n l)"),
                                   c_bank(b, g), ACT.Copy).then_inc(c_copied, 1)

            def silu_u(b):
                act.wait_ge(xc_ready, C2 * (b + 1))
                for c in range(C2):
                    last = act.activation(u[:, b, c, :], ps[:, CONV_BANK[b], c * L:(c + 1) * L], ACT.Silu,
                                          bias=vecs[:, c, CB:CB + 1])
                last.then_inc(u_ready, 1)

            def silu_z(b):
                if b == 0:
                    act.wait_ge(z_stats, 1)
                for c in range(C2):
                    t = 2 * b + c
                    last = act.activation(gz[:, b, c, :], x_sb[:, t, :], ACT.Silu, bias=nmr[:, t, :],
                                          scale=rstd[:, t, :])
                last.then_inc(gz_ready, 1)

            def prep_low(b):
                act.wait_ge(xdbl_ready, b + 1)
                act.activation(dt_low[96:96 + R, b, :], ps[96:96 + R, XDBL_BANK[b], 0:L],
                               ACT.Copy).then_inc(low_ready, 1)

            def prep_soft(b):
                act.wait_ge(dtv_ready, b + 1)
                if b >= 1:
                    act.wait_ge(dt_ready, 2 * b)
                src = ps[:, 0, :] if b == 0 else ps_prep
                for c in range(C2):
                    last = act.activation(dt_abs[:, c, :], src[:, c * L:(c + 1) * L], ACT.Abs,
                                          bias=vecs[:, c, DTB:DTB + 1])
                last.then_inc(act_soft, 1)
                for c in range(C2):
                    last = act.activation(dt_pos[:, c, :], src[:, c * L:(c + 1) * L], ACT.Relu,
                                          bias=vecs[:, c, DTB:DTB + 1])
                last.then_inc(soft_used, 1)
                act.wait_ge(act_soft, 2 * b + 1)
                act.activation(dt_e[:], dt_abs[:], ACT.Exp, scale=-1.0).then_inc(act_soft, 1)
                act.wait_ge(act_soft, 2 * b + 2)
                act.activation(dt_ln[:], dt_e[:], ACT.Ln, bias=1.0).then_inc(soft_ready, 1)

            def decay(s, n0=0, n1=HN):
                b, c, h = step_of(s)
                act.wait_ge(dt_ready, 2 * b + 1)
                if s == 0:
                    act.wait_ge(edges, 1)
                    act.wait_ge(a_ready, 1)
                if s >= 2:
                    act.wait_ge(scan_done, s - 1)
                for n in range(n0, n1):
                    last = act.activation(dA[:, s % 2, n, 1:L], dt[:, b % 2, c, 1:L], ACT.Exp,
                                          scale=a_neg[:, c, h * HN + n:h * HN + n + 1])
                if n1 == HN:
                    last.then_inc(dA_ready, 1)

            def root(var, rstd, ready, done, b):
                act.wait_ge(ready, b + 1)
                act.activation(rstd[:], var[:], ACT.Ln).then_inc(done, 1)
                act.wait_ge(done, 2 * b + 1)
                act.activation(rstd[:], rstd[:], ACT.Exp, scale=-0.5).then_inc(done, 1)

            def exp_router(b):
                act.wait_ge(max_ready, b + 1)
                for lc in range(C2):
                    last = act.activation(ex[:, lc, :], ps_post[:, lc * E:(lc + 1) * E], ACT.Exp,
                                          bias=neg_max[:, lc:lc + 1], accum_out=ex_sum[:, lc:lc + 1])
                last.then_inc(ex_ready, 1)

            act.preload_act_table_set("silu_and_others")
            for c in range(C2):
                act.wait_ge(taps_ready, c + 1)
                act.activation(conv_w[:, c].rearrange("p k m -> p (k m)"), ps[:, 6 + c, :],
                               ACT.Copy).then_inc(conv_w_ready, 1)
            silu_u(0)
            prep_low(0)
            act.preload_act_table_set("natural_log_exp_and_others")
            act.wait_ge(s_small, 32)
            act.activation(a_exp[:], vecs[:, :, AL:AL + NS], ACT.Exp).then_inc(act_seq, 1)
            act.wait_ge(act_seq, 1)
            act.activation(a_neg[:], a_exp[:], ACT.Copy, scale=-1.0).then_inc(a_ready, 1)
            prep_soft(0)
            copy_c(0, 0, 1)
            decay(0)
            copy_c(0, 1, 4)
            root(var, rstd, z_var, z_root, 0)
            decay(1, 0, HN // 2)
            copy_c(0, 4, 6)
            decay(1, HN // 2, HN)
            copy_c(0, 6, 8)
            act.preload_act_table_set("silu_and_others")
            for b in range(1, NB):
                silu_u(b)
            for b in range(1, NB):
                prep_low(b)
            for b in range(NB):
                silu_z(b)
            act.preload_act_table_set("natural_log_exp_and_others")
            for s in range(STEPS):
                b, c, h = step_of(s)
                k = s % SPB
                if b >= 1 and k == 3:
                    exp_router(b - 1)
                if 1 <= s < STEPS - 1:
                    decay(s + 1)
                if b >= 1 and k == 1:
                    root(var2, rstd2, x2_var, x2_root, b - 1)
                if k == 0 and b + 1 < NB:
                    prep_soft(b + 1)
                if b + 1 < NB:
                    copy_c(b + 1, C_GROUPS[k], C_GROUPS[k + 1])
            root(var2, rstd2, x2_var, x2_root, NB - 1)
            exp_router(NB - 1)

            def silu_gate(e, i, g):
                act.wait_ge(gu_ready, e + 1)
                if not (isinstance(e, int) and e < 2):
                    act.wait_ge(mid_ready, e - 1)
                act.activation(sg[:, i % 2, :], ps[:, 2 + i % 2, 0:CAP], ACT.Silu).then_inc(sg_ready, 1)

            def scale_y(e, i, g):
                act.wait_ge(y_ready, e + 1)
                act.wait_ge(ws_ready, e + 1)
                if not (isinstance(g, int) and g == 0):
                    act.wait_ge(added[i], 32 * g)
                for j in range(2):
                    last = act.activation(y_sb[:, i, j, :], ps[0:HALF, 4 + i % 2, j * H:(j + 1) * H],
                                          ACT.Copy, scale=w_slot[:, i, j:j + 1])
                last.then_inc(y_scaled, 1)

            act.wait_ge(flag_ready, 1)
            overflow = act.value_load(flag[0:1, 0:1], min_val=0, max_val=1)
            with act.If(overflow):
                def dense_silu(e):
                    for q in range(2):
                        act.wait_ge(dn_g, 2 * e + q + 1)
                        if not (isinstance(e, int) and e == 0):
                            act.wait_ge(dn_m, 2 * e + q - 1)
                        act.activation(sg_all[:, q, :], ps[:, 2 * q, :], ACT.Silu).then_inc(dn_s, 1)

                dense_silu(0)
                with act.Fori(1, E) as e:
                    dense_silu(e)
            with act.Else():
                for e in range(RING):
                    silu_gate(e, e, 0)
                    if e >= 1:
                        scale_y(e - 1, e - 1, 0)
                with act.Fori(1, E // RING) as g:
                    for i in range(RING):
                        e = g * RING + i
                        silu_gate(e, i, g)
                        scale_y(e - 1, (i - 1) % RING, g if i >= 1 else g - 1)
                scale_y(E - 1, RING - 1, E // RING - 1)

        @block.gpsimd
        def _(pool):
            pool.iota(fill[:, :, ROW - 1].bitcast(U32), [[1, 2]], base=SPARE, channel_multiplier=2).then_inc(fill_made, 1)
            pool.iota(rows[:, :, ROW - 1].bitcast(U32), [[P, NT]], base=0, channel_multiplier=1).then_inc(id_made, 1)

            def soft(b):
                pool.wait_ge(soft_ready, b + 1)
                pool.wait_ge(e1_ready, b)
                pool.tensor_tensor(dt_t[:], dt_e[:], dt_t[:], ALU.subtract).then_inc(pool_seq, 1)
                pool.wait_ge(pool_seq, 2 * b - 1)
                pool.tensor_tensor(dt_t[:], dt_ln[:], dt_t[:], ALU.add).then_inc(pool_seq, 1)
                pool.wait_ge(pool_seq, 2 * b)
                if b >= 2:
                    pool.wait_ge(scan_done, SPB * (b - 1))
                pool.tensor_tensor(dt[:, b % 2], dt_pos[:], dt_t[:], ALU.add).then_inc(dt_ready, 1)
                pool.wait_ge(dt_ready, 2 * b + 1)
                pool.tensor_tensor(du[:, b % 2], dt[:, b % 2], u[:, b], ALU.mult).then_inc(dt_ready, 1)

            def times_c(s):
                b, c, h = step_of(s)
                pool.wait_ge(scan_done, s + 1)
                pool.wait_ge(c_copied, b * HN + (h + 1) * HN // 2)
                n = pool_states(s)
                a = hs[:, s % 2, HN - n:HN, :]
                pool.tensor_tensor(a, a, c_sb[:, b % 2, (h + 1) * HN - n:(h + 1) * HN, :],
                                   ALU.mult).then_inc(hc_pool, 1)

            def send(b, lo, hi):
                if lo == 0:
                    pool.wait_ge(place_ready, b + 1)
                    pool.wait_ge(weights_ready, b + 1)
                    if b == 0:
                        pool.wait_ge(fill_done, 16 * 6)
                        pool.wait_ge(id_made, 2)
                for k in range(lo, hi):
                    t = 2 * b + k // TOPK
                    pool.indirect_dma_start(
                        slots, bass.IndirectOffsetOnAxis(slot_of[:, t, k % TOPK:k % TOPK + 1], 0),
                        rows[:, t, :], None).then_inc(sent, 16)

            pool.memset(tick[:], 0.0).then_inc(id_made, 1)
            for s in range(STEPS):
                b, c, h = step_of(s)
                k = s % SPB
                times_c(s)
                if k == 0 and b + 1 < NB:
                    soft(b + 1)
                if b >= 2:
                    send(b - 2, 4 * k, 4 * k + 4)
            send(NB - 2, 0, 2 * TOPK)
            send(NB - 1, 0, 2 * TOPK)
            pool.wait_ge(sent, 16 * NT * TOPK)
            pool.wait_ge(flag_ready, 1)

            def add_rows(e, i, g):
                pool.wait_ge(y_scaled, e + 1)
                if i >= 2:
                    pool.wait_ge(added[i - 2], 32 * (g + 1))
                elif not (isinstance(g, int) and g == 0):
                    pool.wait_ge(added[i - 2 + RING], 32 * g)
                if not (isinstance(e, int) and e == 0):
                    pool.wait_ge(ticked, e)
                pool.tensor_tensor(tick[:, 1:2], tick[:, 0:1], tick[:, 0:1], ALU.add).then_inc(ticked, 1)
                for j in range(2):
                    pool.indirect_dma_start(
                        sums[i % 2], bass.IndirectOffsetOnAxis(xs[:, i, j, ROW - 1:ROW].bitcast(U32), 0),
                        y_sb[:, i, j, :], None, compute_op=ALU.add).then_inc(added[i], 16)

            overflow = pool.value_load(flag[0:1, 0:1], min_val=0, max_val=1)
            with pool.If(overflow):
                pool.wait_ge(sent, 16 * NT * TOPK)
            with pool.Else():
                for e in range(RING):
                    add_rows(e, e, 0)
                with pool.Fori(1, E // RING) as g:
                    for i in range(RING):
                        add_rows(g * RING + i, i, g)

        @block.vector
        def _(dve):
            seq = [0]

            def link(ins):
                ins.then_inc(dve_seq, 1)
                seq[0] += 1
                dve.wait_ge(dve_seq, seq[0])

            def one_plus(b):
                dve.wait_ge(act_soft, 2 * b + 2)
                if b >= 1:
                    dve.wait_ge(dt_ready, 2 * b)
                return dve.tensor_scalar(dt_t[:], dt_e[:], 1.0, -1.0, ALU.add, ALU.add)

            def first_soft():
                link(one_plus(0))
                link(dve.tensor_tensor(dt_t[:], dt_e[:], dt_t[:], ALU.subtract))
                dve.wait_ge(soft_ready, 1)
                link(dve.tensor_tensor(dt_t[:], dt_ln[:], dt_t[:], ALU.add))
                dve.tensor_tensor(dt[:, 0], dt_pos[:], dt_t[:], ALU.add).then_inc(dt_ready, 1)
                dve.wait_ge(dt_ready, 1)
                dve.tensor_tensor(du[:, 0], dt[:, 0], u[:, 0], ALU.mult).then_inc(dt_ready, 1)

            def prep_parts(b):
                dve.wait_ge(xdbl_ready, b + 1)
                s = bc[:, b, :]
                src = ps[0:96, XDBL_BANK[b], 0:L]
                link(dve.tensor_copy(s, src))
                link(dve.tensor_tensor(bc_rest[:], src, s, ALU.subtract))
                dve.tensor_copy(s[32:64], bc_rest[32:64])
                link(dve.tensor_copy(s[64:96], bc_rest[64:96]))
                dve.tensor_tensor(s[64:96], bc_rest[64:96], s[64:96], ALU.subtract).then_inc(bc_ready, 1)

            def stats(src, st, mv, var):
                for c in range(src.shape[1]):
                    ins = dve.bn_stats(st[:, c, :], src[:, c, :])
                link(ins)
                for c in range(src.shape[1]):
                    ins = dve.bn_aggr(mv[:, c, :], st[:, c, :])
                link(ins)
                return dve.tensor_scalar(var[:], mv[:, :, 1:2], LN_EPS, None, ALU.add)

            def scales(mv, var, rstd, newton, nmr):
                link(dve.tensor_tensor(newton[:], rstd[:], rstd[:], ALU.mult))
                link(dve.tensor_tensor(newton[:], newton[:], var[:], ALU.mult))
                link(dve.tensor_scalar(newton[:], newton[:], -0.5, 1.5, ALU.mult, ALU.add))
                link(dve.tensor_tensor(rstd[:], rstd[:], newton[:], ALU.mult))
                return dve.scalar_tensor_tensor(nmr[:], mv[:, :, 0:1], -1.0, rstd[:], ALU.mult, ALU.mult)

            def step_inputs(s):
                b, c, h = step_of(s)
                dve.wait_ge(dt_ready, 2 * b + 2)
                for q in range(2):
                    dve.wait_ge(b_ready, 2 * s + q + 1)
                    ins = dve.tensor_tensor(
                        dBu[:, 4 * q:4 * q + 4, :], ps_b[q].rearrange("p (n l) -> p n l", n=4),
                        du[:, b % 2, c, :].unsqueeze(1).to_broadcast([P, 4, L]), ALU.mult)
                    ins.then_inc(b_used, 1)

            def scan_step(s):
                dve.wait_ge(b_used, 2 * s + 2)
                dve.wait_ge(dA_ready, s + 1)
                if s >= 2:
                    dve.wait_ge(y_added, s - 1)
                dve.tensor_tensor_scan(
                    hs[:, s % 2].rearrange("p n l -> p (n l)"), dA[:, s % 2].rearrange("p n l -> p (n l)"),
                    dBu[:].rearrange("p n l -> p (n l)"), 0.0, ALU.mult, ALU.add).then_inc(scan_done, 1)

            def times_c(s):
                b, c, h = step_of(s)
                dve.wait_ge(scan_done, s + 1)
                dve.wait_ge(c_copied, b * HN + (h + 1) * HN // 2)
                n = pool_states(s)
                a = hs[:, s % 2, 0:HN - n, :]
                dve.tensor_tensor(a, a, c_sb[:, b % 2, h * HN:(h + 1) * HN - n, :],
                                  ALU.mult).then_inc(hc_dve, 1)

            def gated(b):
                dve.wait_ge(y_added, SPB * (b + 1))
                for c in range(C2):
                    ins = dve.scalar_tensor_tensor(yg[:, c, :], u[:, b, c, :], vecs[:, c, DD:DD + 1],
                                                   ps_y[:, c * L:(c + 1) * L], ALU.mult, ALU.add)
                link(ins)
                dve.wait_ge(gz_ready, b + 1)
                dve.tensor_tensor(yg[:], yg[:], gz[:, b], ALU.mult).then_inc(yg_ready, 1)

            def residual(b):
                dve.wait_ge(yT_ready, b + 1)
                tiles = x2[:, 2 * b:2 * b + 2, :]
                link(dve.tensor_tensor(tiles, ps_post.rearrange("p (t h) -> p t h", h=H),
                                       x_sb[:, 2 * b:2 * b + 2, :], ALU.add))
                stats(tiles, st2, mv2, var2).then_inc(x2_var, 1)

            def norm_h(b):
                dve.wait_ge(x2_root, 2 * b + 2)
                link(scales(mv2, var2, rstd2, newton2, nmr2))
                for lc in range(C2):
                    last = dve.tensor_scalar(rows[:, 2 * b + lc, 0:H], x2[:, 2 * b + lc, :], rstd2[:, lc, :],
                                             nmr2[:, lc, :], ALU.mult, ALU.add)
                last.then_inc(h_ready, 1)

            def copy_hT(b):
                dve.wait_ge(hT_psum, b + 1)
                dve.tensor_copy(hT[:], ps_post.rearrange("p (c l) -> p c l", c=C2)).then_inc(hT_ready, 1)

            def router_max(b):
                dve.wait_ge(logits_ready, b + 1)
                if b >= 1:
                    dve.wait_ge(ex_ready, b)
                dve.tensor_reduce(neg_max[:], ps_post[:, 0:C2 * E].rearrange("p (t e) -> p t e", e=E), AX_X,
                                  ALU.max, negate=True).then_inc(max_ready, 1)

            def choose(b):
                dve.wait_ge(ex_ready, b + 1)
                for t in range(C2):
                    ins = dve.max(top[:, t, :], ex[:, t, :])
                link(ins)
                for t in range(C2):
                    ins = dve.match_replace(rest[:, t, :], top[:, t, :], ex[:, t, :], -1.0)
                link(ins)
                if b >= 1:
                    dve.wait_ge(rank_ready, b)
                dve.tensor_scalar(mask[:], rest[:], 0.0, None, ALU.is_lt).then_inc(mask_ready, 1)
                link(dve.reciprocal(inv_sum[:], ex_sum[:]))
                dve.wait_ge(mask_ready, b + 1)
                for t in range(C2):
                    ins = dve.scalar_tensor_tensor(rows[:, 2 * b + t, H:H + E], ex[:, t, :], inv_sum[:, t:t + 1],
                                                   mask[:, t, :], ALU.mult, ALU.mult)
                ins.then_inc(weights_ready, 1)

            def places(b):
                dve.wait_ge(rank_ready, b + 1)
                rank = ps_post[:, 256:256 + C2 * E]
                dve.scalar_tensor_tensor(r_over[:], rank, float(CAP), place[:, 0, :], ALU.is_ge, ALU.mult)
                dve.scalar_tensor_tensor(r_key[:], rank, -1.0, place[:, 1, :], ALU.mult,
                                         ALU.add).then_inc(rank_used, 1)
                dve.wait_ge(rank_used, b + 1)
                link(dve.tensor_tensor(r_key[:], r_key[:], r_over[:], ALU.subtract))
                link(dve.tensor_tensor(r_key[:], r_key[:], mask[:].rearrange("p t e -> p (t e)"), ALU.mult))
                for t in range(C2):
                    ins = dve.max(key_top[:, t, :], r_key[:, t * E:(t + 1) * E])
                link(ins)
                for t in range(C2):
                    link(dve.tensor_tensor(seen[:], seen[:], mask[:, t, :], ALU.add))
                dve.tensor_scalar(slot_of[:, 2 * b:2 * b + 2, :], key_top[:], -1.0, float(KEY), ALU.mult,
                                  ALU.add).then_inc(place_ready, 1)

            dve.memset(fill[:, :, 0:ROW - 1], 0.0).then_inc(fill_made, 1)
            dve.memset(dA[:, :, :, 0:1], 0.0).then_inc(edges, 1)
            link(dve.memset(seen[:], 0.0))
            dve.wait_ge(s_small, 32)
            for c in range(C2):
                for k in range(KC):
                    ins = dve.tensor_scalar(scaled[:, c, k, :], in_proj[:, c, :], vecs[:, c, k:k + 1], None,
                                            ALU.mult)
                ins.then_inc(scaled_ready, 1)
            dve.wait_ge(s_x, 16)
            stats(x_sb[:], st, mv, var).then_inc(z_var, 1)
            prep_parts(0)
            first_soft()
            for s in range(STEPS):
                b, c, h = step_of(s)
                k = s % SPB
                step_inputs(s)
                if b >= 1 and k == 1:
                    residual(b - 1)
                if b >= 1 and k == 2:
                    copy_hT(b - 1)
                if b >= 1 and k == 3:
                    choose(b - 1)
                if k == 1 and b + 1 < NB:
                    one_plus(b + 1).then_inc(e1_ready, 1)
                if s == 0:
                    dve.wait_ge(z_root, 2)
                    scales(mv, var, rstd, newton, nmr).then_inc(z_stats, 1)
                scan_step(s)
                times_c(s)
                if s == 0:
                    for later in range(1, NB):
                        prep_parts(later)
                if b >= 1 and k == 0:
                    gated(b - 1)
                if b >= 1 and k == 1:
                    norm_h(b - 1)
                if b >= 1 and k == 2:
                    router_max(b - 1)
                if b >= 1 and k == 3:
                    places(b - 1)
            gated(NB - 1)
            residual(NB - 1)
            norm_h(NB - 1)
            copy_hT(NB - 1)
            router_max(NB - 1)
            choose(NB - 1)
            places(NB - 1)
            dve.wait_ge(count_ready, 1)
            link(dve.tensor_reduce(count[:], ps_post[:, 0:E], AX_X, ALU.max))
            dve.tensor_scalar(flag[:], count[:], float(CAP), None, ALU.is_gt).then_inc(flag_ready, 1)

            def copy_rows(e, i, g):
                dve.wait_ge(xT_psum, e + 1)
                if not (isinstance(e, int) and e < 2):
                    dve.wait_ge(gu_ready, e - 1)
                dve.tensor_copy(xT[:, i % 2], ps[:, i % 2, 0:C2 * CAP].rearrange("p (c s) -> p c s", c=C2)
                                ).then_inc(xT_ready, 1)
                col = xs[:, i, :, bass.ds(H + e, 1)].rearrange("p j o -> p (j o)")
                if not (isinstance(g, int) and g == 0):
                    dve.wait_ge(y_scaled, e - RING + 1)
                dve.tensor_copy(w_slot[:, i, :], col).then_inc(ws_ready, 1)

            def middle(e, i, g):
                dve.wait_ge(sg_ready, e + 1)
                if not (isinstance(e, int) and e < 2):
                    dve.wait_ge(y_ready, e - 1)
                dve.tensor_tensor(mid[:, i % 2, :], sg[:, i % 2, :], ps[:, 2 + i % 2, 256:256 + CAP],
                                  ALU.mult).then_inc(mid_ready, 1)

            dve.wait_ge(flag_ready, 1)
            overflow = dve.value_load(flag[0:1, 0:1], min_val=0, max_val=1)
            with dve.If(overflow):
                for t in range(NT):
                    dve.wait_ge(dn_tp, t + 1)
                    dve.tensor_copy(hT_all[:, :, t * P:(t + 1) * P],
                                    ps[:, t % 2, 0:C2 * P].rearrange("p (c m) -> p c m", c=C2)).then_inc(dn_t, 1)

                def dense_sums(e, i):
                    if not isinstance(e, int):
                        dve.wait_ge(dn_acc, 2 * e - 2)
                    dve.tensor_copy(w_tok[:, i, :], rows[:, :, bass.ds(H + e, 1)].rearrange("p t o -> p (t o)")
                                    ).then_inc(dn_wt, 1)
                    for q in range(2):
                        dve.wait_ge(dn_s, 2 * e + q + 1)
                        if not (isinstance(e, int) and e == 0):
                            dve.wait_ge(dn_y, 2 * e + q - 1)
                        dve.tensor_tensor(mid_all[:, q, :], sg_all[:, q, :], ps[:, 2 * q + 1, :],
                                          ALU.mult).then_inc(dn_m, 1)
                    dve.wait_ge(dn_wt, e + 1)
                    for q in range(2):
                        dve.wait_ge(dn_y, 2 * e + q + 1)
                        if not (isinstance(e, int) and e == 0):
                            dve.wait_ge(dn_acc, 2 * e + q - 1)
                        for t in range(NT // 2):
                            tile = x2[:, q * NT // 2 + t, :]
                            k = q * NT // 2 + t
                            ins = dve.scalar_tensor_tensor(
                                tile, ps[:, 4 + 2 * q + t // 2, t % 2 * H:(t % 2 + 1) * H], w_tok[:, i, k:k + 1],
                                tile, ALU.mult, ALU.add)
                        ins.then_inc(dn_acc, 1)

                for i in range(2):
                    dense_sums(i, i)
                with dve.Fori(1, E // 2) as g:
                    for i in range(2):
                        dense_sums(2 * g + i, i)
            with dve.Else():
                for e in range(RING):
                    copy_rows(e, e, 0)
                    if e >= 1:
                        middle(e - 1, e - 1, 0)
                with dve.Fori(1, E // RING) as g:
                    for i in range(RING):
                        e = g * RING + i
                        copy_rows(e, i, g)
                        middle(e - 1, (i - 1) % RING, g if i >= 1 else g - 1)
                middle(E - 1, RING - 1, E // RING - 1)
                for q in range(2):
                    tiles = x2[:, q * (NT // 2):(q + 1) * (NT // 2), :]
                    dve.wait_ge(s_back[q], 32)
                    link(dve.tensor_tensor(tiles, tiles, back[q][:, 0], ALU.add))
                    dve.tensor_tensor(tiles, tiles, back[q][:, 1], ALU.add).then_inc(total_ready, 1)


def layout(inputs):
    a = {k: np.ascontiguousarray(v) for k, v in inputs.items()}
    chunks = lambda w: np.ascontiguousarray(w.reshape(C2, P, -1).transpose(1, 0, 2))
    ctxT = a["ctx_1024"].transpose(2, 0, 1)
    ctxT = np.concatenate([np.zeros((DM, NB, KC - 1), np.float32), ctxT], 2)
    xp = a["L0_xattn_x_proj_w"].T
    bc = xp[:, R:]
    gate, up, down = (a[f"L0_ffn_w_{n}"] for n in ("gate", "up", "down"))
    turned = lambda w: w.transpose(0, 2, 1).reshape(E, C2, P, I).transpose(0, 2, 1, 3).reshape(E, P, C2 * I)
    d = {
        "x": a["x"],
        "ctxT": ctxT,
        "in_proj": chunks(a["L0_xattn_in_proj_w"]),
        "vecs": chunks(np.concatenate([
            a["L0_xattn_conv_w"].reshape(DI, KC), a["L0_xattn_conv_b"][:, None], a["L0_xattn_dt_proj_b"][:, None],
            a["L0_xattn_D"][:, None], a["L0_xattn_A_log"]], 1)),
        "xp_w": chunks(np.concatenate([bc, bc, bc, xp[:, :R]], 1)),
        "dt_wT": a["L0_xattn_dt_proj_w"].T,
        "rt_w": chunks(a["L0_ffn_router_w"].T),
        "w_all": np.concatenate([turned(gate), turned(up), down.transpose(0, 2, 1)], 2),
    }
    d.update(consts())
    return {k: np.ascontiguousarray(v) for k, v in d.items()}


def kernel(**inputs):
    import concourse.bacc as _bacc
    from concourse.bass_utils import run_bass_kernel_spmd as _run

    nc = _bacc.Bacc("TRN2", target_bir_lowering=False, num_devices=1)
    arrays, aps = {}, {}
    for name, v in layout(inputs).items():
        arrays[f"in_{name}"] = v
        aps[name] = nc.dram_tensor(f"in_{name}", v.shape, mybir.dt.from_np(v.dtype), kind="ExternalInput").ap()
    out = nc.dram_tensor("out_0", (NB, L, H), F32, kind="ExternalOutput").ap()
    program(nc, aps, out)
    r = _run(nc, [arrays], core_ids=[0])
    return r.results[0]["out_0"]
```

```python
from contextlib import ExitStack

import numpy as np
import concourse.bass as bass
from concourse import mybir

F32 = mybir.dt.float32
BF16 = mybir.dt.bfloat16
U32 = mybir.dt.uint32
U16 = mybir.dt.uint16
ALU = mybir.AluOpType
ACT = mybir.ActivationFunctionType
AX_X = mybir.AxisListType.X

P = 128
NB, L, DM, DI = 4, 256, 128, 256
H = 256
NS, KC, R = 16, 4, 8
E, TOPK, I = 64, 8, 128
C2 = DI // P
T = NB * L
NT = T // P
HN = NS // 2
STEPS = NB * C2 * 2
SPB = C2 * 2

LN_EPS = 1e-5

C_FIRST = (0, 0, 0, 3, NS // 2)
C_GROUPS = (0, 1, 3, 6, NS // 2)
DVE_FIRST = 2
DVE_SOFT = 2

CONV_BANK = (4, 7, 6, 4)
XDBL_BANK = (6, 7, 6, 7)
DT_BANK = (5, 6, 6, 6)

CAP = 176
HALF = CAP // 2
ROW = H + E + 1
SLOTS = E * CAP
OVER = SLOTS + E * T
KEY = 1 << 17
SPARE = T
SUMS = -(-(T + CAP) // 64) * 64
WROW = 2 * C2 * I + H
RING = 8


def pool_states(s):
    return HN if s < DVE_FIRST else 6 if s < SPB + 2 else 4


def consts():
    one = 0x3F80
    sel = np.zeros((96, 2 * NS, P), np.uint16)
    for j in range(2 * NS):
        for part in range(3):
            sel[32 * part + j, j, :] = one
    ones = np.full((P, P), one, np.uint16)
    tri = np.triu(ones, 1)
    e = np.arange(E)
    over = np.broadcast_to((SLOTS + (T - CAP) * e).astype(np.float32), (P, C2, E))
    base = np.broadcast_to((KEY - CAP * e).astype(np.float32), (P, C2, E))
    return {
        "c_sel": sel.reshape(96, -1),
        "c_tri": np.concatenate([tri, ones], 1),
        "c_ident": np.eye(P, dtype=np.float32),
        "c_place": np.ascontiguousarray(np.stack([over, base], 1).reshape(P, -1)),
    }


def program(nc, d, out):
    with ExitStack() as ctx:
        def sb(name, shape, dt=F32):
            return ctx.enter_context(nc.sbuf_tensor(name, shape, dt))

        def sem(name):
            return ctx.enter_context(nc.semaphore(name))

        ps = ctx.enter_context(nc.psum_tensor("ps", [P, 8, 512], F32))
        ps_b = [ps[:, 2 * q:2 * q + 2, :].rearrange("p a f -> p (a f)") for q in range(2)]
        ps_c, ps_y, ps_prep, ps_post = (ps[:, k, :] for k in (4, 5, 6, 7))

        def c_bank(b, g):
            return (ps_prep if b >= 1 else ps_y) if g % 2 else ps_c

        def copies(b, n):
            return b * HN + n - (HN // 2 if b else 0)

        slots = nc.dram_tensor("slots", (OVER, ROW), F32, kind="Internal").ap()
        sums = [nc.dram_tensor(f"sums{q}", (SUMS, H), F32, kind="Internal").ap() for q in range(2)]

        sel = sb("sel", [96, 2 * NS, P], BF16)
        tri = sb("tri", [P, 2, P], BF16)
        ident = sb("ident", [P, P])
        place = sb("place", [P, 2, C2 * E])
        ctx_pad = sb("ctx_pad", [P, NB, L + KC - 1])
        in_proj = sb("in_proj", [P, C2, DM])
        vecs = sb("vecs", [P, C2, KC + 3 + NS])
        xp_w = sb("xp_w", [P, C2, 104])
        dt_w = sb("dt_w", [104, DI])
        rt_w = sb("rt_w", [P, C2, E])
        scaled = sb("scaled", [P, C2, KC, DM])
        conv_w = sb("conv_w", [P, C2, KC, P])
        d_diag = sb("d_diag", [P, C2, P])
        a_exp = sb("a_exp", [P, C2, NS])
        a_neg = sb("a_neg", [P, C2, NS])
        x_sb = sb("x_sb", [P, NT, H])
        x2 = sb("x2", [P, NT, H])
        rows = sb("rows", [P, NT, ROW])
        hT = sb("hT", [P, C2, L])
        fill = sb("fill", [HALF, 2, ROW])
        u = sb("u", [P, NB, C2, L])
        bc = sb("bc", [96, NB, L], BF16)
        bc_rest = sb("bc_rest", [96, L])
        dt_low = sb("dt_low", [104, NB, L])
        dt_pos = sb("dt_pos", [P, C2, L])
        dt_abs = sb("dt_abs", [P, C2, L])
        dt_e = sb("dt_e", [P, C2, L])
        dt_ln = sb("dt_ln", [P, C2, L])
        dt_t = sb("dt_t", [P, C2, L])
        dt = sb("dt", [P, 2, C2, L])
        du = sb("du", [P, 2, C2, L])
        dA = sb("dA", [P, 2, HN, L])
        dBu = sb("dBu", [P, HN, L])
        hs = sb("hs", [P, 2, HN, L])
        c_sb = sb("c_sb", [P, 2, NS, L])
        st = sb("st", [P, NT, 6])
        mv = sb("mv", [P, NT, 2])
        var = sb("var", [P, NT, 1])
        rstd = sb("rstd", [P, NT, 1])
        newton = sb("newton", [P, NT, 1])
        nmr = sb("nmr", [P, NT, 1])
        gz = sb("gz", [P, NB, C2, L])
        yg = sb("yg", [P, C2, L])
        st2 = sb("st2", [P, C2, 6])
        mv2 = sb("mv2", [P, C2, 2])
        rstd2 = sb("rstd2", [P, C2, 1])
        nmr2 = sb("nmr2", [P, C2, 1])
        var2 = sb("var2", [P, C2, 1])
        newton2 = sb("newton2", [P, C2, 1])
        neg_max = sb("neg_max", [P, C2])
        ex = sb("ex", [P, C2, E])
        ex_sum = sb("ex_sum", [P, C2])
        inv_sum = sb("inv_sum", [P, C2])
        top = sb("top", [P, C2, TOPK])
        rest = sb("rest", [P, C2, E])
        mask = sb("mask", [P, C2, E], BF16)
        seen = sb("seen", [P, E], BF16)
        r_over = sb("r_over", [P, C2 * E])
        r_key = sb("r_key", [P, C2 * E])
        key_top = sb("key_top", [P, C2, TOPK])
        slot_of = sb("slot_of", [P, NT, TOPK], U32)
        count = sb("count", [P, 1])
        flag = sb("flag", [P, 1], U32)
        tick = sb("tick", [P, 2])
        w_ring = sb("w_ring", [P, RING, WROW])
        xs = c_sb[0:HALF].rearrange("p a n l -> p (a n l)")[:, 0:RING * 2 * ROW].rearrange(
            "p (i j f) -> p i j f", i=RING, j=2)
        xT = sb("xT", [P, 2, C2, CAP])
        w_slot = sb("w_slot", [HALF, RING, 2])
        sg = sb("sg", [P, 2, CAP])
        mid = sb("mid", [P, 2, CAP])
        y_sb = hs[0:HALF].rearrange("p a n l -> p (a n l)").rearrange("p (i j h) -> p i j h", i=RING, j=2)
        TH = T // 2
        hT_all = c_sb[:].rearrange("p a n l -> p (a n l)")[:, 0:C2 * T].rearrange("p (c t) -> p c t", c=C2)
        sg_all = c_sb[:].rearrange("p a n l -> p (a n l)")[:, C2 * T:C2 * T + T].rearrange("p (q t) -> p q t", q=2)
        mid_all = c_sb[:].rearrange("p a n l -> p (a n l)")[:, C2 * T + T:C2 * T + 2 * T].rearrange(
            "p (q t) -> p q t", q=2)
        w_tok = sb("w_tok", [P, 2, NT])
        back = [dA[:, q].rearrange("p n l -> p (n l)").rearrange("p (s t h) -> p s t h", s=2, h=H)
                for q in range(2)]

        s_ctx, s_small, s_const, s_x = (sem(n) for n in ("s_ctx", "s_small", "s_const", "s_x"))
        s_router = sem("s_router")
        fill_made, fill_done = sem("fill_made"), sem("fill_done")
        id_made = sem("id_made")
        diag_ready = sem("diag_ready")
        edges = sem("edges")
        dve_seq = sem("dve_seq")
        scaled_ready, taps_ready, conv_w_ready = sem("scaled_ready"), sem("taps_ready"), sem("conv_w_ready")
        act_seq, a_ready, s_ident = sem("act_seq"), sem("a_ready"), sem("s_ident")
        xc_ready, u_ready = sem("xc_ready"), sem("u_ready")
        xdbl_ready, low_ready, bc_ready, dtv_ready = (
            sem(n) for n in ("xdbl_ready", "low_ready", "bc_ready", "dtv_ready"))
        act_soft, soft_used, soft_ready, pool_seq, dt_ready = (
            sem(n) for n in ("act_soft", "soft_used", "soft_ready", "pool_seq", "dt_ready"))
        dA_ready, scan_done = sem("dA_ready"), sem("scan_done")
        b_ready, b_used, c_ready, c_copied, c_late = (
            sem(n) for n in ("b_ready", "b_used", "c_ready", "c_copied", "c_late"))
        hc_pool, hc_dve, y_added = sem("hc_pool"), sem("hc_dve"), sem("y_added")
        z_stats, gz_ready = sem("z_stats"), sem("gz_ready")
        e1_ready = sem("e1_ready")
        z_var, z_root, x2_var, x2_root = (
            sem(n) for n in ("z_var", "z_root", "x2_var", "x2_root"))
        yg_ready, yT_ready, x2_stats, h_ready, hT_psum, hT_ready, logits_ready = (
            sem(n) for n in ("yg_ready", "yT_ready", "x2_stats", "h_ready", "hT_psum", "hT_ready", "logits_ready"))
        max_ready, ex_ready, mask_ready, rank_ready, rank_used, place_ready = (
            sem(n) for n in ("max_ready", "ex_ready", "mask_ready", "rank_ready", "rank_used", "place_ready"))
        ticked = sem("ticked")
        weights_ready = sem("weights_ready")
        sent, last_sent = sem("sent"), [sem(f"last_sent{k}") for k in range(TOPK)]
        count_ready, flag_ready = sem("count_ready"), sem("flag_ready")
        w_loaded = [sem(f"w_loaded{i}") for i in range(RING)]
        xs_loaded = [sem(f"xs_loaded{i}") for i in range(RING)]
        added = [sem(f"added{i}") for i in range(RING)]
        xT_psum, xT_ready, gu_ready, sg_ready, mid_ready, y_ready, y_scaled, ws_ready = (
            sem(n) for n in ("xT_psum", "xT_ready", "gu_ready", "sg_ready", "mid_ready", "y_ready", "y_scaled", "ws_ready"))
        s_back, total_ready, s_out = [sem(f"s_back{i}") for i in range(2)], sem("total_ready"), sem("s_out")
        dn_w = [sem(f"dn_w{i}") for i in range(2)]
        dn_tp, dn_t, dn_wt, dn_g, dn_s, dn_m, dn_y, dn_acc = (
            sem(n) for n in ("dn_tp", "dn_t", "dn_wt", "dn_g", "dn_s", "dn_m", "dn_y", "dn_acc"))

        CB, DTB, DD, AL = KC, KC + 1, KC + 2, KC + 3
        expert_w = d["w_all"]
        slot_view = slots[0:SLOTS, :].rearrange("(e p j) f -> e p j f", p=HALF, j=2)
        out_rows = out.rearrange("b l h -> (b l) h").rearrange("(t p) h -> p t h", p=P)
        x_rows = d["x"].rearrange("b l h -> (b l) h").rearrange("(t p) h -> p t h", p=P)

        def step_of(s):
            return s // SPB, (s // 2) % C2, s % 2

        block = ctx.enter_context(nc.Block())

        @block.sync
        def _(sp):
            for name, tile in (("in_proj", in_proj), ("vecs", vecs)):
                sp.dma_start(tile[:], d[name]).then_inc(s_small, 16)
            sp.dma_start(ctx_pad[:], d["ctxT"]).then_inc(s_ctx, 16)
            sp.dma_start(ident[:], d["c_ident"]).then_inc(s_ident, 16)
            sp.dma_start(xp_w[:], d["xp_w"]).then_inc(s_const, 16)
            sp.dma_start(dt_w[96:104, :], d["dt_wT"]).then_inc(s_const, 16)
            sp.dma_start(sel[:].bitcast(U16), d["c_sel"].rearrange("k (j m) -> k j m", m=P)).then_inc(s_const, 16)
            sp.dma_start(x_sb[:], x_rows).then_inc(s_x, 16)
            sp.dma_start(rt_w[:], d["rt_w"]).then_inc(s_router, 16)
            sp.dma_start(tri[:].bitcast(U16), d["c_tri"].rearrange("p (a m) -> p a m", a=2)).then_inc(s_router, 16)
            sp.dma_start(place[:], d["c_place"].rearrange("p (a m) -> p a m", a=2)).then_inc(s_router, 16)
            sp.wait_ge(fill_made, 2)
            for q in range(4):
                n = E // 4
                src = fill[:].rearrange("p j f -> p (j f)").unsqueeze(1).to_broadcast([HALF, n, 2 * ROW])
                sp.dma_start(slot_view[q * n:(q + 1) * n].rearrange("e p j f -> p e (j f)"),
                             src).then_inc(fill_done, 16)
            for s in range(2):
                sp.dma_start(sums[s].rearrange("(r p) h -> p r h", p=64),
                             fill[0:64, 0, 0:H].unsqueeze(1).to_broadcast([64, SUMS // 64, H]),
                             ).then_inc(fill_done, 16)
            for i in range(RING):
                sp.dma_start(w_ring[:, i, :], expert_w[i]).then_inc(w_loaded[i], 16)

            sp.wait_ge(flag_ready, 1)
            overflow = sp.value_load(flag[0:1, 0:1], min_val=0, max_val=1)
            with sp.If(overflow):
                for i in range(RING):
                    sp.wait_ge(w_loaded[i], 16)

                def load_dense(e, i):
                    if not isinstance(e, int):
                        sp.wait_ge(dn_y, 2 * e - 2)
                    sp.dma_start(w_ring[:, i, :], expert_w[bass.ds(e, 1)].rearrange("e p w -> (e p) w")
                                 ).then_inc(dn_w[i], 16)

                for i in range(2):
                    load_dense(i, i)
                with sp.Fori(1, E // 2) as g:
                    for i in range(2):
                        load_dense(2 * g + i, i)
                sp.wait_ge(dn_acc, 2 * E)
                sp.dma_start(out_rows, x2[:]).then_inc(s_out, 16)
                sp.wait_ge(s_out, 16)
            with sp.Else():
                sp.wait_ge(sent, 16 * (NT - C2) * TOPK)

                def load(e, i, g):
                    if g is not None:
                        sp.wait_ge(y_ready, e - RING + 1)
                        sp.dma_start(w_ring[:, i, :], expert_w[bass.ds(e, 1)].rearrange("e p w -> (e p) w")
                                     ).then_inc(w_loaded[i], 16)
                        sp.wait_ge(added[i], 32 * g)
                    elif e < TOPK:
                        sp.wait_ge(last_sent[e], 16 * C2)
                    src = slot_view[bass.ds(e, 1)] if g is not None else slot_view[e:e + 1]
                    sp.dma_start(xs[:, i, :, :], src.rearrange("e p j f -> (e p) j f")).then_inc(xs_loaded[i], 16)

                for i in range(RING):
                    load(i, i, None)
                with sp.Fori(1, E // RING) as g:
                    for i in range(RING):
                        load(g * RING + i, i, g)
                for i in range(RING):
                    sp.wait_ge(added[i], 32 * (E // RING))
                for q in range(2):
                    for s in range(2):
                        src = sums[s][q * (T // 2):(q + 1) * (T // 2), :].rearrange("(t p) h -> p t h", p=P)
                        sp.dma_start(back[q][:, s], src).then_inc(s_back[q], 16)
                for q in range(2):
                    sp.wait_ge(total_ready, q + 1)
                    sp.dma_start(out_rows[:, q * (NT // 2):(q + 1) * (NT // 2), :],
                                 x2[:, q * (NT // 2):(q + 1) * (NT // 2), :]).then_inc(s_out, 16)
                sp.wait_ge(s_out, 32)

        @block.tensor
        def _(pe):
            def bank_of(b):
                return ps[:, CONV_BANK[b], :]

            def prep_x(b, c):
                if b == 2 and c == 0:
                    pe.wait_ge(bc_ready, 1)
                    pe.wait_ge(low_ready, 1)
                if b == 3 and c == 0:
                    pe.wait_ge(c_late, HN // 2)
                for k in range(KC):
                    mm = pe.matmul(bank_of(b)[:, c * L:(c + 1) * L], conv_w[:, c, k, :],
                                   ctx_pad[:, b, k:k + L], start=(k == 0), stop=(k == KC - 1))
                mm.then_inc(xc_ready, 1)

            def prep_bc(b):
                pe.wait_ge(u_ready, b + 1)
                if b == 0:
                    pe.wait_ge(s_const, 16 * 3)
                if b == 3:
                    pe.wait_ge(bc_ready, 2)
                    pe.wait_ge(low_ready, 2)
                o = ps[0:104, XDBL_BANK[b], 0:L]
                for c in range(C2):
                    mm = pe.matmul(o, xp_w[:, c, :], u[:, b, c, :], start=(c == 0), stop=(c == C2 - 1))
                mm.then_inc(xdbl_ready, 1)

            def prep_dt(b):
                if b == 0:
                    pe.wait_ge(low_ready, 1)
                elif b == 1:
                    pe.wait_ge(low_ready, 3)
                    pe.wait_ge(bc_ready, 3)
                else:
                    pe.wait_ge(c_copied, copies(b, 0))
                o = ps[:, DT_BANK[b], :]
                for c in range(C2):
                    mm = pe.matmul(o[:, c * L:(c + 1) * L], dt_w[96:96 + R, c * P:(c + 1) * P],
                                   dt_low[96:96 + R, b, :], start=True, stop=True)
                mm.then_inc(dtv_ready, 1)

            def spread_b(s, q):
                b, c, h = step_of(s)
                pe.wait_ge(bc_ready, b + 1)
                if s >= 1:
                    pe.wait_ge(b_used, 2 * (s - 1) + q + 1)
                for k in range(4):
                    mm = pe.matmul(ps_b[q][:, k * L:(k + 1) * L], sel[:, h * HN + 4 * q + k, :],
                                   bc[:, b, :], start=True, stop=True)
                mm.then_inc(b_ready, 1)

            def spread_c(b, n0, n1):
                for g in range(n0, n1):
                    pe.wait_ge(bc_ready, b + 1)
                    if b == 0:
                        if g == 1:
                            pe.wait_ge(soft_used, 1)
                        if 2 <= g < 6:
                            pe.wait_ge(c_copied, g - 1)
                        if g >= 6:
                            pe.wait_ge(c_late, g - 5)
                    elif b >= 1:
                        pe.wait_ge(c_copied, copies(b, max(g - 1, 0)))
                        if b == 1 and g == 0:
                            pe.wait_ge(u_ready, NB)
                        if g == 1:
                            pe.wait_ge(soft_used, b + 1)
                    for k in range(2):
                        mm = pe.matmul(c_bank(b, g)[:, k * L:(k + 1) * L], sel[:, NS + 2 * g + k, :],
                                       bc[:, b, :], start=True, stop=True)
                    mm.then_inc(c_ready, 1)

            def add_states(s, half):
                b, c, h = step_of(s)
                if half == 0:
                    if s == 0:
                        pe.wait_ge(c_late, HN // 2)
                        pe.wait_ge(diag_ready, 1)
                    if c == 0 and h == 0 and b >= 1:
                        pe.wait_ge(yg_ready, b)
                    if h == 0:
                        pe.matmul(ps_y[:, c * L:(c + 1) * L], d_diag[:, c, :], u[:, b, c, :], start=True, stop=False)
                    if s >= DVE_FIRST:
                        pe.wait_ge(hc_dve, s + 1 - DVE_FIRST)
                if half == 1 or pool_states(s) > HN // 2:
                    pe.wait_ge(hc_pool, s + 1)
                for n in range(half * HN // 2, (half + 1) * HN // 2):
                    mm = pe.matmul(ps_y[:, c * L:(c + 1) * L], ident[:], hs[:, s % 2, n, :],
                                   start=False, stop=(h == 1 and n == HN - 1))
                if half == 1:
                    mm.then_inc(y_added, 1)

            def turn_y(b):
                pe.wait_ge(yg_ready, b + 1)
                if b >= 1:
                    pe.wait_ge(rank_used, b)
                else:
                    pe.wait_ge(low_ready, 4)
                    pe.wait_ge(bc_ready, 4)
                for c in range(C2):
                    for lc in range(C2):
                        mm = pe.transpose(ps_post[:, lc * H + c * P:lc * H + (c + 1) * P],
                                          yg[:, c, lc * P:(lc + 1) * P], ident[:])
                mm.then_inc(yT_ready, 1)

            def turn_h(b):
                pe.wait_ge(h_ready, b + 1)
                for lc in range(C2):
                    for c in range(C2):
                        mm = pe.transpose(ps_post[:, c * L + lc * P:c * L + (lc + 1) * P],
                                          rows[:, 2 * b + lc, c * P:(c + 1) * P], ident[:])
                mm.then_inc(hT_psum, 1)

            def router(b):
                pe.wait_ge(hT_ready, b + 1)
                if b == 0:
                    pe.wait_ge(s_router, 16 * 3)
                for lc in range(C2):
                    for c in range(C2):
                        mm = pe.matmul(ps_post[:, lc * E:(lc + 1) * E],
                                       hT[:, c, lc * P:(lc + 1) * P], rt_w[:, c, :],
                                       start=(c == 0), stop=(c == C2 - 1))
                mm.then_inc(logits_ready, 1)

            def ranks(b):
                pe.wait_ge(mask_ready, b + 1)
                strict, ones = tri[:, 0, :], tri[:, 1, :]
                for lc in range(C2):
                    o = ps_post[:, 256 + lc * E:256 + (lc + 1) * E]
                    pe.matmul(o, strict, mask[:, lc, :], start=True, stop=False)
                    mm = pe.matmul(o, ones, seen[:], start=False, stop=(lc == 0))
                    if lc:
                        mm = pe.matmul(o, ones, mask[:, 0, :], start=False, stop=True)
                mm.then_inc(rank_ready, 1)

            pe.wait_ge(scaled_ready, 2)
            pe.wait_ge(s_ident, 16)
            for c in range(C2):
                for k in range(KC):
                    mm = pe.transpose(ps[:, 6 + c, k * P:(k + 1) * P], scaled[:, c, k, :], ident[:])
                mm.then_inc(taps_ready, 1)
            pe.wait_ge(conv_w_ready, 2)
            pe.wait_ge(s_ctx, 16)
            for c in range(C2):
                prep_x(0, c)
            prep_bc(0)
            prep_dt(0)
            spread_b(0, 0)
            spread_b(0, 1)
            spread_c(0, 0, 1)
            prep_x(1, 0)
            spread_c(0, 1, 2)
            prep_x(1, 1)
            spread_c(0, 2, 4)
            prep_x(2, 0)
            prep_x(2, 1)
            for s in range(STEPS):
                b, c, h = step_of(s)
                k = s % SPB
                groups = C_FIRST if b == 0 else C_GROUPS
                if b >= 1 and k == 1:
                    turn_y(b - 1)
                if s == 1:
                    spread_b(2, 0)
                    spread_b(2, 1)
                    spread_c(0, 6, 8)
                if s >= 1:
                    add_states(s - 1, 0)
                if s == 2:
                    prep_dt(1)
                if s != 1 and s + 1 < STEPS:
                    spread_b(s + 1, 0)
                if b >= 1 and k == 2:
                    turn_h(b - 1)
                if s >= 1:
                    add_states(s - 1, 1)
                if s != 1 and s + 1 < STEPS:
                    spread_b(s + 1, 1)
                if b >= 1 and k == 2:
                    router(b - 1)
                if b >= 1 and k == 3:
                    ranks(b - 1)
                if s == 0:
                    spread_c(0, 4, 6)
                if s == 1:
                    prep_bc(1)
                    prep_bc(2)
                    prep_x(3, 0)
                    prep_x(3, 1)
                if 1 <= b < NB - 1 and k == 0:
                    prep_dt(b + 1)
                if s == 2:
                    prep_bc(3)
                if b + 1 < NB:
                    spread_c(b + 1, groups[k], groups[k + 1])
            for half in range(2):
                add_states(STEPS - 1, half)
            turn_y(NB - 1)
            turn_h(NB - 1)
            router(NB - 1)
            ranks(NB - 1)
            pe.wait_ge(place_ready, NB)
            pe.matmul(ps_post[:, 0:E], tri[:, 1, :], seen[:], start=True, stop=True).then_inc(count_ready, 1)

            def turn(e, i, g):
                pe.wait_ge(xs_loaded[i], 16 * (g + 1))
                if not (isinstance(e, int) and e < 2):
                    pe.wait_ge(xT_ready, e - 1)
                for j in range(2):
                    for c in range(C2):
                        mm = pe.transpose(ps[:, i % 2, c * CAP + j * HALF:c * CAP + (j + 1) * HALF],
                                          xs[:, i, j, c * P:(c + 1) * P], ident[0:HALF, 0:HALF])
                mm.then_inc(xT_psum, 1)

            def gate_up(e, i, g):
                pe.wait_ge(w_loaded[i], 16 * (g + 1))
                pe.wait_ge(xT_ready, e + 1)
                if not (isinstance(e, int) and e < 2):
                    pe.wait_ge(mid_ready, e - 1)
                for m in range(2):
                    for c in range(C2):
                        w = w_ring[:, i, (m * C2 + c) * I:(m * C2 + c + 1) * I]
                        mm = pe.matmul(ps[:, 2 + i % 2, m * 256:m * 256 + CAP], w, xT[:, i % 2, c, :],
                                       start=(c == 0), stop=(c == C2 - 1))
                mm.then_inc(gu_ready, 1)

            def down(e, i, g):
                pe.wait_ge(mid_ready, e + 1)
                if not (isinstance(e, int) and e < 2):
                    pe.wait_ge(y_scaled, e - 1)
                for j in range(2):
                    mm = pe.matmul(ps[0:HALF, 4 + i % 2, j * H:(j + 1) * H],
                                   mid[:, i % 2, j * HALF:(j + 1) * HALF], w_ring[:, i, 2 * C2 * I:WROW],
                                   start=True, stop=True)
                mm.then_inc(y_ready, 1)

            pe.wait_ge(flag_ready, 1)
            overflow = pe.value_load(flag[0:1, 0:1], min_val=0, max_val=1)
            with pe.If(overflow):
                for t in range(NT):
                    if t >= 2:
                        pe.wait_ge(dn_t, t - 1)
                    for c in range(C2):
                        mm = pe.transpose(ps[:, t % 2, c * P:(c + 1) * P], rows[:, t, c * P:(c + 1) * P], ident[:])
                    mm.then_inc(dn_tp, 1)
                pe.wait_ge(dn_t, NT)

                def dense_expert(e, i, g):
                    pe.wait_ge(dn_w[i], 16 * (g + 1))
                    for q in range(2):
                        if not (isinstance(e, int) and e == 0):
                            pe.wait_ge(dn_m, 2 * e + q - 1)
                        for m in range(2):
                            for c in range(C2):
                                w = w_ring[:, i, (m * C2 + c) * I:(m * C2 + c + 1) * I]
                                mm = pe.matmul(ps[:, 2 * q + m, :], w, hT_all[:, c, q * TH:(q + 1) * TH],
                                               start=(c == 0), stop=(c == C2 - 1))
                        mm.then_inc(dn_g, 1)
                    for q in range(2):
                        pe.wait_ge(dn_m, 2 * e + q + 1)
                        if not (isinstance(e, int) and e == 0):
                            pe.wait_ge(dn_acc, 2 * e + q - 1)
                        for t in range(NT // 2):
                            mm = pe.matmul(ps[:, 4 + 2 * q + t // 2, t % 2 * H:(t % 2 + 1) * H],
                                           mid_all[:, q, t * P:(t + 1) * P], w_ring[:, i, 2 * C2 * I:WROW],
                                           start=True, stop=True)
                        mm.then_inc(dn_y, 1)

                for i in range(2):
                    dense_expert(i, i, 0)
                with pe.Fori(1, E // 2) as g:
                    for i in range(2):
                        dense_expert(2 * g + i, i, g)
            with pe.Else():
                for e in range(RING):
                    turn(e, e, 0)
                    if e >= 1:
                        gate_up(e - 1, e - 1, 0)
                    if e >= 2:
                        down(e - 2, e - 2, 0)
                with pe.Fori(1, E // RING) as g:
                    for i in range(RING):
                        e = g * RING + i
                        turn(e, i, g)
                        gate_up(e - 1, (i - 1) % RING, g if i >= 1 else g - 1)
                        down(e - 2, (i - 2) % RING, g if i >= 2 else g - 1)
                gate_up(E - 1, RING - 1, E // RING - 1)
                down(E - 2, RING - 2, E // RING - 1)
                down(E - 1, RING - 1, E // RING - 1)

        @block.scalar
        def _(act):
            def copy_c(b, n0, n1):
                for g in range(n0, n1):
                    if g == 0 and b >= 2:
                        act.wait_ge(hc_pool, SPB * (b - 1))
                        act.wait_ge(hc_dve, SPB * (b - 1) - DVE_FIRST)
                    act.wait_ge(c_ready, b * HN + g + 1)
                    act.activation(c_sb[:, b % 2, 2 * g:2 * g + 2, :].rearrange("p n l -> p (n l)"),
                                   c_bank(b, g), ACT.Copy).then_inc(c_copied, 1)

            def silu_u(b):
                act.wait_ge(xc_ready, C2 * (b + 1))
                for c in range(C2):
                    last = act.activation(u[:, b, c, :], ps[:, CONV_BANK[b], c * L:(c + 1) * L], ACT.Silu,
                                          bias=vecs[:, c, CB:CB + 1])
                last.then_inc(u_ready, 1)

            def silu_z(b):
                if b == 0:
                    act.wait_ge(z_stats, 1)
                for c in range(C2):
                    t = 2 * b + c
                    last = act.activation(gz[:, b, c, :], x_sb[:, t, :], ACT.Silu, bias=nmr[:, t, :],
                                          scale=rstd[:, t, :])
                last.then_inc(gz_ready, 1)

            def prep_low(b):
                act.wait_ge(xdbl_ready, b + 1)
                act.activation(dt_low[96:96 + R, b, :], ps[96:96 + R, XDBL_BANK[b], 0:L],
                               ACT.Copy).then_inc(low_ready, 1)

            def prep_soft(b):
                act.wait_ge(dtv_ready, b + 1)
                if b >= 1:
                    act.wait_ge(dt_ready, 2 * b)
                src = ps[:, DT_BANK[b], :]
                for c in range(C2):
                    last = act.activation(dt_abs[:, c, :], src[:, c * L:(c + 1) * L], ACT.Abs,
                                          bias=vecs[:, c, DTB:DTB + 1])
                last.then_inc(act_soft, 1)
                for c in range(C2):
                    last = act.activation(dt_pos[:, c, :], src[:, c * L:(c + 1) * L], ACT.Relu,
                                          bias=vecs[:, c, DTB:DTB + 1])
                last.then_inc(soft_used, 1)
                act.wait_ge(act_soft, 2 * b + 1)
                act.activation(dt_e[:], dt_abs[:], ACT.Exp, scale=-1.0).then_inc(act_soft, 1)
                act.wait_ge(act_soft, 2 * b + 2)
                act.activation(dt_ln[:], dt_e[:], ACT.Ln, bias=1.0).then_inc(soft_ready, 1)

            def decay(s, n0=0, n1=HN):
                b, c, h = step_of(s)
                act.wait_ge(dt_ready, 2 * b + 1)
                if s == 0:
                    act.wait_ge(edges, 1)
                    act.wait_ge(a_ready, 1)
                if s >= 2:
                    act.wait_ge(scan_done, s - 1)
                for n in range(n0, n1):
                    last = act.activation(dA[:, s % 2, n, 1:L], dt[:, b % 2, c, 1:L], ACT.Exp,
                                          scale=a_neg[:, c, h * HN + n:h * HN + n + 1])
                if n1 == HN:
                    last.then_inc(dA_ready, 1)

            def root(var, rstd, ready, done, b):
                act.wait_ge(ready, b + 1)
                act.activation(rstd[:], var[:], ACT.Ln).then_inc(done, 1)
                act.wait_ge(done, 2 * b + 1)
                act.activation(rstd[:], rstd[:], ACT.Exp, scale=-0.5).then_inc(done, 1)

            def norm_h(b):
                act.wait_ge(x2_stats, b + 1)
                for lc in range(C2):
                    last = act.activation(rows[:, 2 * b + lc, 0:H], x2[:, 2 * b + lc, :], ACT.Identity,
                                          bias=nmr2[:, lc, :], scale=rstd2[:, lc, :])
                last.then_inc(h_ready, 1)

            def copy_hT(b):
                act.wait_ge(hT_psum, b + 1)
                act.activation(hT[:], ps_post.rearrange("p (c l) -> p c l", c=C2),
                               ACT.Copy).then_inc(hT_ready, 1)

            def exp_router(b):
                act.wait_ge(max_ready, b + 1)
                for lc in range(C2):
                    last = act.activation(ex[:, lc, :], ps_post[:, lc * E:(lc + 1) * E], ACT.Exp,
                                          bias=neg_max[:, lc:lc + 1], accum_out=ex_sum[:, lc:lc + 1])
                last.then_inc(ex_ready, 1)

            act.preload_act_table_set("silu_and_others")
            for c in range(C2):
                act.wait_ge(taps_ready, c + 1)
                act.activation(conv_w[:, c].rearrange("p k m -> p (k m)"), ps[:, 6 + c, :],
                               ACT.Copy).then_inc(conv_w_ready, 1)
            silu_u(0)
            prep_low(0)
            act.preload_act_table_set("natural_log_exp_and_others")
            act.wait_ge(s_small, 32)
            act.activation(a_exp[:], vecs[:, :, AL:AL + NS], ACT.Exp).then_inc(act_seq, 1)
            act.wait_ge(act_seq, 1)
            act.activation(a_neg[:], a_exp[:], ACT.Copy, scale=-1.0).then_inc(a_ready, 1)
            prep_soft(0)
            root(var, rstd, z_var, z_root, 0)
            copy_c(0, 0, 2)
            decay(0)
            copy_c(0, 2, 3)
            decay(1)
            copy_c(0, 3, 4)
            decay(2)
            decay(3)
            act.preload_act_table_set("silu_and_others")
            silu_u(1)
            silu_u(2)
            prep_low(1)
            prep_low(2)
            silu_z(0)
            silu_z(1)
            silu_z(2)
            silu_z(3)
            silu_u(3)
            act.preload_act_table_set("natural_log_exp_and_others")
            for s in range(2, STEPS):
                b, c, h = step_of(s)
                k = s % SPB
                groups = C_FIRST if b == 0 else C_GROUPS
                if b >= 1 and k == 2:
                    norm_h(b - 1)
                if s == 2:
                    prep_soft(1)
                    prep_low(3)
                if 3 <= s < STEPS - 1:
                    decay(s + 1, 0, HN // 2)
                if b >= 1 and k == 2:
                    copy_hT(b - 1)
                if 3 <= s < STEPS - 1:
                    decay(s + 1, HN // 2, HN)
                if b >= 1 and k == 2:
                    exp_router(b - 1)
                if b >= 1 and k == 1:
                    root(var2, rstd2, x2_var, x2_root, b - 1)
                if 1 <= b < NB - 1 and k == 0:
                    prep_soft(b + 1)
                if b + 1 < NB:
                    copy_c(b + 1, groups[k], groups[k + 1])
            root(var2, rstd2, x2_var, x2_root, NB - 1)
            norm_h(NB - 1)
            copy_hT(NB - 1)
            exp_router(NB - 1)

            def silu_gate(e, i, g):
                act.wait_ge(gu_ready, e + 1)
                if not (isinstance(e, int) and e < 2):
                    act.wait_ge(mid_ready, e - 1)
                act.activation(sg[:, i % 2, :], ps[:, 2 + i % 2, 0:CAP], ACT.Silu).then_inc(sg_ready, 1)

            def scale_y(e, i, g):
                act.wait_ge(y_ready, e + 1)
                act.wait_ge(ws_ready, e + 1)
                if not (isinstance(g, int) and g == 0):
                    act.wait_ge(added[i], 32 * g)
                for j in range(2):
                    last = act.activation(y_sb[:, i, j, :], ps[0:HALF, 4 + i % 2, j * H:(j + 1) * H],
                                          ACT.Copy, scale=w_slot[:, i, j:j + 1])
                last.then_inc(y_scaled, 1)

            act.wait_ge(flag_ready, 1)
            overflow = act.value_load(flag[0:1, 0:1], min_val=0, max_val=1)
            with act.If(overflow):
                def dense_silu(e):
                    for q in range(2):
                        act.wait_ge(dn_g, 2 * e + q + 1)
                        if not (isinstance(e, int) and e == 0):
                            act.wait_ge(dn_m, 2 * e + q - 1)
                        act.activation(sg_all[:, q, :], ps[:, 2 * q, :], ACT.Silu).then_inc(dn_s, 1)

                dense_silu(0)
                with act.Fori(1, E) as e:
                    dense_silu(e)
            with act.Else():
                for e in range(RING):
                    silu_gate(e, e, 0)
                    if e >= 1:
                        scale_y(e - 1, e - 1, 0)
                with act.Fori(1, E // RING) as g:
                    for i in range(RING):
                        e = g * RING + i
                        silu_gate(e, i, g)
                        scale_y(e - 1, (i - 1) % RING, g if i >= 1 else g - 1)
                scale_y(E - 1, RING - 1, E // RING - 1)

        @block.gpsimd
        def _(pool):
            pool.iota(fill[:, :, ROW - 1].bitcast(U32), [[1, 2]], base=SPARE, channel_multiplier=2).then_inc(fill_made, 1)
            pool.iota(rows[:, :, ROW - 1].bitcast(U32), [[P, NT]], base=0, channel_multiplier=1).then_inc(id_made, 1)

            def soft(b, half):
                mine = b - DVE_SOFT
                if half == 0:
                    pool.wait_ge(soft_ready, b + 1)
                    pool.wait_ge(e1_ready, mine + 1)
                    pool.tensor_tensor(dt_t[:], dt_e[:], dt_t[:], ALU.subtract).then_inc(pool_seq, 1)
                    pool.wait_ge(pool_seq, 2 * mine + 1)
                    pool.tensor_tensor(dt_t[:], dt_ln[:], dt_t[:], ALU.add).then_inc(pool_seq, 1)
                else:
                    pool.wait_ge(pool_seq, 2 * mine + 2)
                    pool.wait_ge(scan_done, SPB * (b - 1))
                    pool.tensor_tensor(dt[:, b % 2], dt_pos[:], dt_t[:], ALU.add).then_inc(dt_ready, 1)
                    pool.wait_ge(dt_ready, 2 * b + 1)
                    pool.tensor_tensor(du[:, b % 2], dt[:, b % 2], u[:, b], ALU.mult).then_inc(dt_ready, 1)

            def times_c(s):
                b, c, h = step_of(s)
                pool.wait_ge(scan_done, s + 1)
                if b == 0 and h == 1:
                    pool.wait_ge(c_late, HN // 2)
                else:
                    pool.wait_ge(c_copied, copies(b, h * HN // 2 + HN // 2))
                n = pool_states(s)
                a = hs[:, s % 2, HN - n:HN, :]
                pool.tensor_tensor(a, a, c_sb[:, b % 2, (h + 1) * HN - n:(h + 1) * HN, :],
                                   ALU.mult).then_inc(hc_pool, 1)

            def send(b, lo, hi):
                if lo == 0:
                    pool.wait_ge(place_ready, b + 1)
                    pool.wait_ge(weights_ready, b + 1)
                    if b == 0:
                        pool.wait_ge(fill_done, 16 * 6)
                        pool.wait_ge(id_made, 2)
                for k in range(lo, hi):
                    t = 2 * b + k // TOPK
                    pool.indirect_dma_start(
                        slots, bass.IndirectOffsetOnAxis(slot_of[:, t, k % TOPK:k % TOPK + 1], 0),
                        rows[:, t, :], None).then_inc(sent, 16)

            pool.memset(tick[:], 0.0).then_inc(id_made, 1)
            for s in range(STEPS):
                b, c, h = step_of(s)
                k = s % SPB
                times_c(s)
                if k in (1, 2) and DVE_SOFT <= b + 1 < NB:
                    soft(b + 1, k - 1)
                if b >= 2:
                    send(b - 2, 4 * k, 4 * k + 4)
            send(NB - 2, 0, 2 * TOPK)
            pool.wait_ge(flag_ready, 1)

            def send_last():
                pool.wait_ge(place_ready, NB)
                pool.wait_ge(weights_ready, NB)
                for k in range(TOPK):
                    for t in range(NT - C2, NT):
                        pool.indirect_dma_start(
                            slots, bass.IndirectOffsetOnAxis(slot_of[:, t, k:k + 1], 0),
                            rows[:, t, :], None).then_inc(last_sent[k], 16)

            def add_rows(e, i, g):
                pool.wait_ge(y_scaled, e + 1)
                if i >= 2:
                    pool.wait_ge(added[i - 2], 32 * (g + 1))
                elif not (isinstance(g, int) and g == 0):
                    pool.wait_ge(added[i - 2 + RING], 32 * g)
                if not (isinstance(e, int) and e == 0):
                    pool.wait_ge(ticked, e)
                pool.tensor_tensor(tick[:, 1:2], tick[:, 0:1], tick[:, 0:1], ALU.add).then_inc(ticked, 1)
                for j in range(2):
                    pool.indirect_dma_start(
                        sums[i % 2], bass.IndirectOffsetOnAxis(xs[:, i, j, ROW - 1:ROW].bitcast(U32), 0),
                        y_sb[:, i, j, :], None, compute_op=ALU.add).then_inc(added[i], 16)

            overflow = pool.value_load(flag[0:1, 0:1], min_val=0, max_val=1)
            with pool.If(overflow):
                pool.wait_ge(sent, 16 * (NT - C2) * TOPK)
            with pool.Else():
                send_last()
                for e in range(RING):
                    add_rows(e, e, 0)
                with pool.Fori(1, E // RING) as g:
                    for i in range(RING):
                        add_rows(g * RING + i, i, g)

        @block.vector
        def _(dve):
            seq = [0]

            def link(ins):
                ins.then_inc(dve_seq, 1)
                seq[0] += 1
                dve.wait_ge(dve_seq, seq[0])

            def one_plus(b):
                dve.wait_ge(act_soft, 2 * b + 2)
                if b >= 1:
                    dve.wait_ge(dt_ready, 2 * b)
                return dve.tensor_scalar(dt_t[:], dt_e[:], 1.0, -1.0, ALU.add, ALU.add)

            def soft(b):
                link(one_plus(b))
                link(dve.tensor_tensor(dt_t[:], dt_e[:], dt_t[:], ALU.subtract))
                dve.wait_ge(soft_ready, b + 1)
                link(dve.tensor_tensor(dt_t[:], dt_ln[:], dt_t[:], ALU.add))
                dve.tensor_tensor(dt[:, b], dt_pos[:], dt_t[:], ALU.add).then_inc(dt_ready, 1)
                dve.wait_ge(dt_ready, 2 * b + 1)
                dve.tensor_tensor(du[:, b], dt[:, b], u[:, b], ALU.mult).then_inc(dt_ready, 1)

            def prep_parts(b):
                dve.wait_ge(xdbl_ready, b + 1)
                s = bc[:, b, :]
                src = ps[0:96, XDBL_BANK[b], 0:L]
                link(dve.tensor_copy(s, src))
                link(dve.tensor_tensor(bc_rest[:], src, s, ALU.subtract))
                dve.tensor_copy(s[32:64], bc_rest[32:64])
                link(dve.tensor_copy(s[64:96], bc_rest[64:96]))
                dve.tensor_tensor(s[64:96], bc_rest[64:96], s[64:96], ALU.subtract).then_inc(bc_ready, 1)

            def stats(src, st, mv, var):
                for c in range(src.shape[1]):
                    ins = dve.bn_stats(st[:, c, :], src[:, c, :])
                link(ins)
                for c in range(src.shape[1]):
                    ins = dve.bn_aggr(mv[:, c, :], st[:, c, :])
                link(ins)
                return dve.tensor_scalar(var[:], mv[:, :, 1:2], LN_EPS, None, ALU.add)

            def scales(mv, var, rstd, newton, nmr):
                link(dve.tensor_tensor(newton[:], rstd[:], rstd[:], ALU.mult))
                link(dve.tensor_tensor(newton[:], newton[:], var[:], ALU.mult))
                link(dve.tensor_scalar(newton[:], newton[:], -0.5, 1.5, ALU.mult, ALU.add))
                link(dve.tensor_tensor(rstd[:], rstd[:], newton[:], ALU.mult))
                return dve.scalar_tensor_tensor(nmr[:], mv[:, :, 0:1], -1.0, rstd[:], ALU.mult, ALU.mult)

            def step_inputs(s):
                b, c, h = step_of(s)
                dve.wait_ge(dt_ready, 2 * b + 2)
                for q in range(2):
                    dve.wait_ge(b_ready, 2 * s + q + 1)
                    ins = dve.tensor_tensor(
                        dBu[:, 4 * q:4 * q + 4, :], ps_b[q].rearrange("p (n l) -> p n l", n=4),
                        du[:, b % 2, c, :].unsqueeze(1).to_broadcast([P, 4, L]), ALU.mult)
                    ins.then_inc(b_used, 1)

            def scan_step(s):
                dve.wait_ge(b_used, 2 * s + 2)
                dve.wait_ge(dA_ready, s + 1)
                if s >= 2:
                    dve.wait_ge(y_added, s - 1)
                dve.tensor_tensor_scan(
                    hs[:, s % 2].rearrange("p n l -> p (n l)"), dA[:, s % 2].rearrange("p n l -> p (n l)"),
                    dBu[:].rearrange("p n l -> p (n l)"), 0.0, ALU.mult, ALU.add).then_inc(scan_done, 1)

            def copy_c(g):
                dve.wait_ge(c_ready, g + 1)
                dve.tensor_copy(c_sb[:, 0, 2 * g:2 * g + 2, :].rearrange("p n l -> p (n l)"),
                                c_bank(0, g)).then_inc(c_late, 1)

            def times_c(s):
                b, c, h = step_of(s)
                dve.wait_ge(scan_done, s + 1)
                if b == 0 and h == 1:
                    dve.wait_ge(c_late, HN // 2)
                else:
                    dve.wait_ge(c_copied, copies(b, h * HN // 2 + HN // 2))
                n = pool_states(s)
                a = hs[:, s % 2, 0:HN - n, :]
                dve.tensor_tensor(a, a, c_sb[:, b % 2, h * HN:(h + 1) * HN - n, :],
                                  ALU.mult).then_inc(hc_dve, 1)

            def gated(b):
                dve.wait_ge(y_added, SPB * (b + 1))
                dve.wait_ge(gz_ready, b + 1)
                dve.tensor_tensor(yg[:], ps_y.rearrange("p (c l) -> p c l", c=C2), gz[:, b],
                                  ALU.mult).then_inc(yg_ready, 1)

            def residual(b):
                dve.wait_ge(yT_ready, b + 1)
                tiles = x2[:, 2 * b:2 * b + 2, :]
                link(dve.tensor_tensor(tiles, ps_post.rearrange("p (t h) -> p t h", h=H),
                                       x_sb[:, 2 * b:2 * b + 2, :], ALU.add))
                if b >= 1:
                    dve.wait_ge(h_ready, b)
                stats(tiles, st2, mv2, var2).then_inc(x2_var, 1)

            def x2_scales(b):
                dve.wait_ge(x2_root, 2 * b + 2)
                scales(mv2, var2, rstd2, newton2, nmr2).then_inc(x2_stats, 1)

            def router_max(b):
                dve.wait_ge(logits_ready, b + 1)
                if b >= 1:
                    dve.wait_ge(ex_ready, b)
                dve.tensor_reduce(neg_max[:], ps_post[:, 0:C2 * E].rearrange("p (t e) -> p t e", e=E), AX_X,
                                  ALU.max, negate=True).then_inc(max_ready, 1)

            def choose(b):
                dve.wait_ge(ex_ready, b + 1)
                for t in range(C2):
                    ins = dve.max(top[:, t, :], ex[:, t, :])
                link(ins)
                for t in range(C2):
                    ins = dve.match_replace(rest[:, t, :], top[:, t, :], ex[:, t, :], -1.0)
                link(ins)
                if b >= 1:
                    dve.wait_ge(rank_ready, b)
                dve.tensor_scalar(mask[:], rest[:], 0.0, None, ALU.is_lt).then_inc(mask_ready, 1)
                link(dve.reciprocal(inv_sum[:], ex_sum[:]))
                dve.wait_ge(mask_ready, b + 1)
                for t in range(C2):
                    ins = dve.scalar_tensor_tensor(rows[:, 2 * b + t, H:H + E], ex[:, t, :], inv_sum[:, t:t + 1],
                                                   mask[:, t, :], ALU.mult, ALU.mult)
                ins.then_inc(weights_ready, 1)

            def places(b):
                dve.wait_ge(rank_ready, b + 1)
                rank = ps_post[:, 256:256 + C2 * E]
                dve.scalar_tensor_tensor(r_over[:], rank, float(CAP), place[:, 0, :], ALU.is_ge, ALU.mult)
                dve.scalar_tensor_tensor(r_key[:], rank, -1.0, place[:, 1, :], ALU.mult,
                                         ALU.add).then_inc(rank_used, 1)
                dve.wait_ge(rank_used, b + 1)
                link(dve.tensor_tensor(r_key[:], r_key[:], r_over[:], ALU.subtract))
                link(dve.tensor_tensor(r_key[:], r_key[:], mask[:].rearrange("p t e -> p (t e)"), ALU.mult))
                for t in range(C2):
                    ins = dve.max(key_top[:, t, :], r_key[:, t * E:(t + 1) * E])
                link(ins)
                for t in range(C2):
                    link(dve.tensor_tensor(seen[:], seen[:], mask[:, t, :], ALU.add))
                dve.tensor_scalar(slot_of[:, 2 * b:2 * b + 2, :], key_top[:], -1.0, float(KEY), ALU.mult,
                                  ALU.add).then_inc(place_ready, 1)

            dve.memset(fill[:, :, 0:ROW - 1], 0.0).then_inc(fill_made, 1)
            dve.memset(dA[:, :, :, 0:1], 0.0).then_inc(edges, 1)
            link(dve.memset(seen[:], 0.0))
            dve.wait_ge(s_small, 32)
            for c in range(C2):
                for k in range(KC):
                    ins = dve.tensor_scalar(scaled[:, c, k, :], in_proj[:, c, :], vecs[:, c, k:k + 1], None,
                                            ALU.mult)
                ins.then_inc(scaled_ready, 1)
            dve.wait_ge(s_ident, 16)
            for c in range(C2):
                ins = dve.tensor_scalar(d_diag[:, c, :], ident[:], vecs[:, c, DD:DD + 1], None, ALU.mult)
            ins.then_inc(diag_ready, 1)
            dve.wait_ge(s_x, 16)
            stats(x_sb[:], st, mv, var).then_inc(z_var, 1)
            prep_parts(0)
            soft(0)
            for s in range(STEPS):
                b, c, h = step_of(s)
                k = s % SPB
                step_inputs(s)
                if b >= 1 and k == 1:
                    residual(b - 1)
                if b >= 1 and k == 3:
                    choose(b - 1)
                if k == 1 and DVE_SOFT <= b + 1 < NB:
                    one_plus(b + 1).then_inc(e1_ready, 1)
                scan_step(s)
                if s >= DVE_FIRST:
                    times_c(s)
                if s == 0:
                    dve.wait_ge(z_root, 2)
                    scales(mv, var, rstd, newton, nmr).then_inc(z_stats, 1)
                if s == 1:
                    for g in range(HN // 2, HN):
                        copy_c(g)
                if s == 2:
                    prep_parts(1)
                    prep_parts(2)
                if s == 3:
                    prep_parts(3)
                    soft(1)
                if b >= 1 and k == 0:
                    gated(b - 1)
                if b >= 1 and k == 1:
                    x2_scales(b - 1)
                if b >= 1 and k == 2:
                    router_max(b - 1)
                if b >= 1 and k == 3:
                    places(b - 1)
            gated(NB - 1)
            residual(NB - 1)
            x2_scales(NB - 1)
            router_max(NB - 1)
            choose(NB - 1)
            places(NB - 1)
            dve.wait_ge(count_ready, 1)
            link(dve.tensor_reduce(count[:], ps_post[:, 0:E], AX_X, ALU.max))
            dve.tensor_scalar(flag[:], count[:], float(CAP), None, ALU.is_gt).then_inc(flag_ready, 1)

            def copy_rows(e, i, g):
                dve.wait_ge(xT_psum, e + 1)
                if not (isinstance(e, int) and e < 2):
                    dve.wait_ge(gu_ready, e - 1)
                dve.tensor_copy(xT[:, i % 2], ps[:, i % 2, 0:C2 * CAP].rearrange("p (c s) -> p c s", c=C2)
                                ).then_inc(xT_ready, 1)
                col = xs[:, i, :, bass.ds(H + e, 1)].rearrange("p j o -> p (j o)")
                if not (isinstance(g, int) and g == 0):
                    dve.wait_ge(y_scaled, e - RING + 1)
                dve.tensor_copy(w_slot[:, i, :], col).then_inc(ws_ready, 1)

            def middle(e, i, g):
                dve.wait_ge(sg_ready, e + 1)
                if not (isinstance(e, int) and e < 2):
                    dve.wait_ge(y_ready, e - 1)
                dve.tensor_tensor(mid[:, i % 2, :], sg[:, i % 2, :], ps[:, 2 + i % 2, 256:256 + CAP],
                                  ALU.mult).then_inc(mid_ready, 1)

            dve.wait_ge(flag_ready, 1)
            overflow = dve.value_load(flag[0:1, 0:1], min_val=0, max_val=1)
            with dve.If(overflow):
                for t in range(NT):
                    dve.wait_ge(dn_tp, t + 1)
                    dve.tensor_copy(hT_all[:, :, t * P:(t + 1) * P],
                                    ps[:, t % 2, 0:C2 * P].rearrange("p (c m) -> p c m", c=C2)).then_inc(dn_t, 1)

                def dense_sums(e, i):
                    if not isinstance(e, int):
                        dve.wait_ge(dn_acc, 2 * e - 2)
                    dve.tensor_copy(w_tok[:, i, :], rows[:, :, bass.ds(H + e, 1)].rearrange("p t o -> p (t o)")
                                    ).then_inc(dn_wt, 1)
                    for q in range(2):
                        dve.wait_ge(dn_s, 2 * e + q + 1)
                        if not (isinstance(e, int) and e == 0):
                            dve.wait_ge(dn_y, 2 * e + q - 1)
                        dve.tensor_tensor(mid_all[:, q, :], sg_all[:, q, :], ps[:, 2 * q + 1, :],
                                          ALU.mult).then_inc(dn_m, 1)
                    dve.wait_ge(dn_wt, e + 1)
                    for q in range(2):
                        dve.wait_ge(dn_y, 2 * e + q + 1)
                        if not (isinstance(e, int) and e == 0):
                            dve.wait_ge(dn_acc, 2 * e + q - 1)
                        for t in range(NT // 2):
                            tile = x2[:, q * NT // 2 + t, :]
                            k = q * NT // 2 + t
                            ins = dve.scalar_tensor_tensor(
                                tile, ps[:, 4 + 2 * q + t // 2, t % 2 * H:(t % 2 + 1) * H], w_tok[:, i, k:k + 1],
                                tile, ALU.mult, ALU.add)
                        ins.then_inc(dn_acc, 1)

                for i in range(2):
                    dense_sums(i, i)
                with dve.Fori(1, E // 2) as g:
                    for i in range(2):
                        dense_sums(2 * g + i, i)
            with dve.Else():
                for e in range(RING):
                    copy_rows(e, e, 0)
                    if e >= 1:
                        middle(e - 1, e - 1, 0)
                with dve.Fori(1, E // RING) as g:
                    for i in range(RING):
                        e = g * RING + i
                        copy_rows(e, i, g)
                        middle(e - 1, (i - 1) % RING, g if i >= 1 else g - 1)
                middle(E - 1, RING - 1, E // RING - 1)
                for q in range(2):
                    tiles = x2[:, q * (NT // 2):(q + 1) * (NT // 2), :]
                    dve.wait_ge(s_back[q], 32)
                    link(dve.tensor_tensor(tiles, tiles, back[q][:, 0], ALU.add))
                    dve.tensor_tensor(tiles, tiles, back[q][:, 1], ALU.add).then_inc(total_ready, 1)


def layout(inputs):
    a = {k: np.ascontiguousarray(v) for k, v in inputs.items()}
    chunks = lambda w: np.ascontiguousarray(w.reshape(C2, P, -1).transpose(1, 0, 2))
    ctxT = a["ctx_1024"].transpose(2, 0, 1)
    ctxT = np.concatenate([np.zeros((DM, NB, KC - 1), np.float32), ctxT], 2)
    xp = a["L0_xattn_x_proj_w"].T
    bc = xp[:, R:]
    gate, up, down = (a[f"L0_ffn_w_{n}"] for n in ("gate", "up", "down"))
    turned = lambda w: w.transpose(0, 2, 1).reshape(E, C2, P, I).transpose(0, 2, 1, 3).reshape(E, P, C2 * I)
    d = {
        "x": a["x"],
        "ctxT": ctxT,
        "in_proj": chunks(a["L0_xattn_in_proj_w"]),
        "vecs": chunks(np.concatenate([
            a["L0_xattn_conv_w"].reshape(DI, KC), a["L0_xattn_conv_b"][:, None], a["L0_xattn_dt_proj_b"][:, None],
            a["L0_xattn_D"][:, None], a["L0_xattn_A_log"]], 1)),
        "xp_w": chunks(np.concatenate([bc, bc, bc, xp[:, :R]], 1)),
        "dt_wT": a["L0_xattn_dt_proj_w"].T,
        "rt_w": chunks(a["L0_ffn_router_w"].T),
        "w_all": np.concatenate([turned(gate), turned(up), down.transpose(0, 2, 1)], 2),
    }
    d.update(consts())
    return {k: np.ascontiguousarray(v) for k, v in d.items()}


def kernel(**inputs):
    import concourse.bacc as _bacc
    from concourse.bass_utils import run_bass_kernel_spmd as _run

    nc = _bacc.Bacc("TRN2", target_bir_lowering=False, num_devices=1)
    arrays, aps = {}, {}
    for name, v in layout(inputs).items():
        arrays[f"in_{name}"] = v
        aps[name] = nc.dram_tensor(f"in_{name}", v.shape, mybir.dt.from_np(v.dtype), kind="ExternalInput").ap()
    out = nc.dram_tensor("out_0", (NB, L, H), F32, kind="ExternalOutput").ap()
    program(nc, aps, out)
    r = _run(nc, [arrays], core_ids=[0])
    return r.results[0]["out_0"]
```

```python
from contextlib import ExitStack

import numpy as np
import concourse.bass as bass
from concourse import mybir

F32 = mybir.dt.float32
F32R = mybir.dt.float32r
BF16 = mybir.dt.bfloat16
U32 = mybir.dt.uint32
U16 = mybir.dt.uint16
ALU = mybir.AluOpType
ACT = mybir.ActivationFunctionType
AX_X = mybir.AxisListType.X

P = 128
NB, L, DM, DI = 4, 256, 128, 256
H = 256
NS, KC, R = 16, 4, 8
E, TOPK, I = 64, 8, 128
C2 = DI // P
T = NB * L
NT = T // P
HN = NS // 2
STEPS = NB * C2 * 2
SPB = C2 * 2

LN_EPS = 1e-5

C_FIRST = (0, 0, 0, 0, 6)
C_GROUPS = (0, 0, 2, 4, NS // 2)
SENDS = (4, 8, 12, 2 * TOPK)
POOL_STATES = (4, 4, 6, 6, 6, 4, 4, 5, 5, 4, 4, 5, 5, 5, 5, 4)
DVE_SOFT = 2

CONV_BANK = (4, 7, 6, 5)
XDBL_BANK = (6, 7, 6, 7)
DT_BANK = (5, 4, 6, 6)

CAP = 176
HALF = CAP // 2
ROW = H + E + 1
SLOTS = E * CAP
OVER = SLOTS + E * T
KEY = 1 << 17
SPARE = T
SUMS = -(-(T + CAP) // 64) * 64
SETS = 3
SET_OF = (0, 1, 2, 0, 1, 2, 0, 1)
SET_LAST = (2, 0, 1, 2, 0, 1, 0, 1)
DONE_AT = {s: max(i for i in range(8) if SET_LAST[i] == s) for s in range(SETS)}
BACK = 4
WROW = 2 * C2 * I + H
RING = 8


def consts():
    one = 0x3F80
    sel = np.zeros((96, 2 * NS, P), np.uint16)
    for j in range(2 * NS):
        for part in range(3):
            sel[32 * part + j, j, :] = one
    ones = np.full((P, P), one, np.uint16)
    tri = np.triu(ones, 1)
    e = np.arange(E)
    over = np.broadcast_to((SLOTS + (T - CAP) * e).astype(np.float32), (P, C2, E))
    base = np.broadcast_to((KEY - CAP * e).astype(np.float32), (P, C2, E))
    return {
        "c_sel": sel.reshape(96, -1),
        "c_tri": np.concatenate([tri, ones], 1),
        "c_ident": np.eye(P, dtype=np.float32),
        "c_place": np.ascontiguousarray(np.stack([over, base], 1).reshape(P, -1)),
    }


def program(nc, d, out):
    with ExitStack() as ctx:
        def sb(name, shape, dt=F32):
            return ctx.enter_context(nc.sbuf_tensor(name, shape, dt))

        def sem(name):
            return ctx.enter_context(nc.semaphore(name))

        ps = ctx.enter_context(nc.psum_tensor("ps", [P, 8, 512], F32))
        ps_b = [ps[:, 2 * q:2 * q + 2, :].rearrange("p a f -> p (a f)") for q in range(2)]
        ps_c, ps_y, ps_prep, ps_post = (ps[:, k, :] for k in (4, 5, 6, 7))

        def c_bank(b, g):
            return ps_c if g % 2 == 0 or b == 0 and g >= HN // 2 else ps_prep if b >= 1 else ps_y

        def copies(b, n):
            return b * HN + n - (2 if b or n > 4 else 0)

        slots = nc.dram_tensor("slots", (OVER, ROW), F32, kind="Internal").ap()
        sums = [nc.dram_tensor(f"sums{q}", (SUMS, H), F32, kind="Internal").ap() for q in range(SETS)]

        sel = sb("sel", [96, 2 * NS, P], BF16)
        tri = sb("tri", [P, 2, P], BF16)
        ident = sb("ident", [P, P])
        place = sb("place", [P, 2, C2 * E])
        ctx_pad = sb("ctx_pad", [P, NB, L + KC - 1])
        vecs = sb("vecs", [P, C2, 3 + NS])
        xp_w = sb("xp_w", [P, C2, 104])
        dt_w = sb("dt_w", [104, DI])
        rt_w = sb("rt_w", [P, C2, E])
        conv_w = sb("conv_w", [P, C2, KC, P])
        d_diag = sb("d_diag", [P, C2, P])
        a_exp = sb("a_exp", [P, C2, NS])
        a_neg = sb("a_neg", [P, C2, NS])
        x_sb = sb("x_sb", [P, NT, H])
        x2 = sb("x2", [P, NT, H])
        rows = sb("rows", [P, NT, ROW])
        hT = sb("hT", [P, C2, L])
        fill = sb("fill", [HALF, 2, ROW])
        u = sb("u", [P, NB, C2, L])
        bc = sb("bc", [96, NB, L], BF16)
        bc_rest = sb("bc_rest", [96, L])
        dt_low = sb("dt_low", [104, NB, L])
        dt_pos = sb("dt_pos", [P, C2, L])
        dt_abs = sb("dt_abs", [P, C2, L])
        dt_e = sb("dt_e", [P, C2, L])
        dt_ln = sb("dt_ln", [P, C2, L])
        dt_t = sb("dt_t", [P, C2, L])
        dt = sb("dt", [P, 2, C2, L])
        du = sb("du", [P, 2, C2, L])
        dA = sb("dA", [P, 2, HN, L])
        dBu = sb("dBu", [P, HN, L])
        hs = sb("hs", [P, 2, HN, L])
        c_sb = sb("c_sb", [P, 2, NS, L])
        taps = hs[:, 0, 0:KC, :]
        in_proj = hs[:, 0, KC, :]
        st = sb("st", [P, NT, 6])
        mv = sb("mv", [P, NT, 2])
        var = sb("var", [P, NT, 1])
        rstd = sb("rstd", [P, NT, 1])
        newton = sb("newton", [P, NT, 1])
        nmr = sb("nmr", [P, NT, 1])
        gz = sb("gz", [P, NB, C2, L])
        yg = sb("yg", [P, C2, L])
        st2 = sb("st2", [P, C2, 6])
        mv2 = sb("mv2", [P, C2, 2])
        rstd2 = sb("rstd2", [P, C2, 1])
        nmr2 = sb("nmr2", [P, C2, 1])
        var2 = sb("var2", [P, C2, 1])
        newton2 = sb("newton2", [P, C2, 1])
        neg_max = sb("neg_max", [P, C2])
        ex = sb("ex", [P, C2, E])
        ex_sum = sb("ex_sum", [P, C2])
        inv_sum = sb("inv_sum", [P, C2])
        top = sb("top", [P, C2, TOPK])
        rest = sb("rest", [P, C2, E])
        mask = sb("mask", [P, NB, C2, E], BF16)
        r_over = sb("r_over", [P, C2 * E])
        r_key = sb("r_key", [P, C2 * E])
        key_top = sb("key_top", [P, C2, TOPK])
        slot_of = sb("slot_of", [P, NT, TOPK], U32)
        count = sb("count", [P, 1])
        flag = sb("flag", [P, 1], U32)
        tick = sb("tick", [P, 2])
        w_ring = sb("w_ring", [P, RING, WROW])
        xs = c_sb[0:HALF].rearrange("p a n l -> p (a n l)")[:, 0:RING * 2 * ROW].rearrange(
            "p (i j f) -> p i j f", i=RING, j=2)
        xT = sb("xT", [P, 2, C2, CAP])
        w_slot = sb("w_slot", [HALF, RING, 2])
        sg = sb("sg", [P, 2, CAP])
        mid = sb("mid", [P, 2, CAP])
        mid_hl = sb("mid_hl", [P, 2, 2, CAP], F32R)
        down_hl = sb("down_hl", [P, 2, 2, H], F32R)
        y_sb = hs[0:HALF].rearrange("p a n l -> p (a n l)").rearrange("p (i j h) -> p i j h", i=RING, j=2)
        TH = T // 2
        hT_all = c_sb[:].rearrange("p a n l -> p (a n l)")[:, 0:C2 * T].rearrange("p (c t) -> p c t", c=C2)
        sg_all = c_sb[:].rearrange("p a n l -> p (a n l)")[:, C2 * T:C2 * T + T].rearrange("p (q t) -> p q t", q=2)
        mid_all = c_sb[:].rearrange("p a n l -> p (a n l)")[:, C2 * T + T:C2 * T + 2 * T].rearrange(
            "p (q t) -> p q t", q=2)
        w_tok = key_top[:]
        back = {2: dA[:, 0].rearrange("p n l -> p (n l)").rearrange("p (t h) -> p t h", h=H),
                0: dA[:, 1].rearrange("p n l -> p (n l)").rearrange("p (t h) -> p t h", h=H),
                1: x_sb[:]}

        s_ctx, s_small, s_const, s_x = (sem(n) for n in ("s_ctx", "s_small", "s_const", "s_x"))
        s_router, s_taps, s_ctx_rest = sem("s_router"), sem("s_taps"), sem("s_ctx_rest")
        fill_made, fill_done = sem("fill_made"), sem("fill_done")
        id_made = sem("id_made")
        diag_ready = sem("diag_ready")
        edges = sem("edges")
        dve_seq = sem("dve_seq")
        conv_w_ready, conv_saved = sem("conv_w_ready"), sem("conv_saved")
        act_seq, a_ready, s_ident = sem("act_seq"), sem("a_ready"), sem("s_ident")
        xc_ready, u_ready = sem("xc_ready"), sem("u_ready")
        xdbl_ready, low_ready, bc_ready, dtv_ready = (
            sem(n) for n in ("xdbl_ready", "low_ready", "bc_ready", "dtv_ready"))
        act_soft, soft_used, soft_ready, pool_seq, dt_ready = (
            sem(n) for n in ("act_soft", "soft_used", "soft_ready", "pool_seq", "dt_ready"))
        dA_ready, scan_done = sem("dA_ready"), sem("scan_done")
        b_ready, b_used, c_ready, c_copied, c_late = (
            sem(n) for n in ("b_ready", "b_used", "c_ready", "c_copied", "c_late"))
        hc_pool, hc_dve, y_added = sem("hc_pool"), sem("hc_dve"), sem("y_added")
        z_stats, gz_ready = sem("z_stats"), sem("gz_ready")
        e1_ready = sem("e1_ready")
        z_var, z_root, x2_var, x2_root = (
            sem(n) for n in ("z_var", "z_root", "x2_var", "x2_root"))
        yg_ready, yT_ready, x2_stats, h_ready, hT_psum, hT_ready, logits_ready = (
            sem(n) for n in ("yg_ready", "yT_ready", "x2_stats", "h_ready", "hT_psum", "hT_ready", "logits_ready"))
        max_ready, ex_ready, mask_ready, rank_ready, rank_used, place_ready = (
            sem(n) for n in ("max_ready", "ex_ready", "mask_ready", "rank_ready", "rank_used", "place_ready"))
        ticked, high_ready, split_ready = sem("ticked"), sem("high_ready"), sem("split_ready")
        weights_ready = sem("weights_ready")
        sent, last_sent = sem("sent"), [sem(f"last_sent{k}") for k in range(TOPK)]
        count_ready, flag_ready = sem("count_ready"), sem("flag_ready")
        w_loaded = [sem(f"w_loaded{i}") for i in range(RING)]
        xs_loaded = [sem(f"xs_loaded{i}") for i in range(RING)]
        added = [sem(f"added{i}") for i in range(RING)]
        xT_psum, xT_ready, gu_ready, sg_ready, mid_ready, y_ready, y_scaled, ws_ready = (
            sem(n) for n in ("xT_psum", "xT_ready", "gu_ready", "sg_ready", "mid_ready", "y_ready", "y_scaled", "ws_ready"))
        s_back = {s: [sem(f"s_back{s}_{q}") for q in range(BACK)] for s in range(SETS)}
        total_ready, s_out = sem("total_ready"), sem("s_out")
        dn_w = [sem(f"dn_w{i}") for i in range(2)]
        dn_tp, dn_t, dn_wt, dn_g, dn_s, dn_m, dn_y, dn_acc = (
            sem(n) for n in ("dn_tp", "dn_t", "dn_wt", "dn_g", "dn_s", "dn_m", "dn_y", "dn_acc"))

        CB, DTB, DD, AL = 0, 1, 2, 3
        expert_w = d["w_all"]
        slot_view = slots[0:SLOTS, :].rearrange("(e p j) f -> e p j f", p=HALF, j=2)
        out_rows = out.rearrange("b l h -> (b l) h").rearrange("(t p) h -> p t h", p=P)
        x_rows = d["x"].rearrange("b l h -> (b l) h").rearrange("(t p) h -> p t h", p=P)

        def step_of(s):
            return s // SPB, (s // 2) % C2, s % 2

        block = ctx.enter_context(nc.Block())

        @block.sync
        def _(sp):
            sp.dma_start(in_proj, d["in_projT"]).then_inc(s_taps, 16)
            sp.dma_start(taps, d["taps"].to_broadcast([P, KC, DI])).then_inc(s_taps, 16)
            sp.dma_start(ctx_pad[:, 0, :], d["ctxT"][:, 0, :]).then_inc(s_ctx, 16)
            sp.dma_start(vecs[:], d["vecs"]).then_inc(s_small, 16)
            sp.dma_start(xp_w[:], d["xp_w"]).then_inc(s_const, 16)
            sp.dma_start(dt_w[96:104, :], d["dt_wT"]).then_inc(s_const, 16)
            sp.dma_start(x_sb[:], x_rows).then_inc(s_x, 16)
            sp.dma_start(ident[:], d["c_ident"]).then_inc(s_ident, 16)
            sp.dma_start(sel[:].bitcast(U16), d["c_sel"].rearrange("k (j m) -> k j m", m=P)).then_inc(s_const, 16)
            sp.dma_start(ctx_pad[:, 1:, :], d["ctxT"][:, 1:, :]).then_inc(s_ctx_rest, 16)
            sp.dma_start(rt_w[:], d["rt_w"]).then_inc(s_router, 16)
            sp.dma_start(tri[:].bitcast(U16), d["c_tri"].rearrange("p (a m) -> p a m", a=2)).then_inc(s_router, 16)
            sp.dma_start(place[:], d["c_place"].rearrange("p (a m) -> p a m", a=2)).then_inc(s_router, 16)
            sp.wait_ge(fill_made, 2)
            for q in range(4):
                n = E // 4
                src = fill[:].rearrange("p j f -> p (j f)").unsqueeze(1).to_broadcast([HALF, n, 2 * ROW])
                sp.dma_start(slot_view[q * n:(q + 1) * n].rearrange("e p j f -> p e (j f)"),
                             src).then_inc(fill_done, 16)
            for s in range(SETS):
                sp.dma_start(sums[s].rearrange("(r p) h -> p r h", p=64),
                             fill[0:64, 0, 0:H].unsqueeze(1).to_broadcast([64, SUMS // 64, H]),
                             ).then_inc(fill_done, 16)
            for i in range(RING):
                sp.dma_start(w_ring[:, i, :], expert_w[i]).then_inc(w_loaded[i], 16)

            sp.wait_ge(flag_ready, 1)
            overflow = sp.value_load(flag[0:1, 0:1], min_val=0, max_val=1)
            with sp.If(overflow):
                for i in range(RING):
                    sp.wait_ge(w_loaded[i], 16)

                def load_dense(e, i):
                    if not isinstance(e, int):
                        sp.wait_ge(dn_y, 2 * e - 2)
                    sp.dma_start(w_ring[:, i, :], expert_w[bass.ds(e, 1)].rearrange("e p w -> (e p) w")
                                 ).then_inc(dn_w[i], 16)

                for i in range(2):
                    load_dense(i, i)
                with sp.Fori(1, E // 2) as g:
                    for i in range(2):
                        load_dense(2 * g + i, i)
                sp.wait_ge(dn_acc, 2 * E)
                sp.dma_start(out_rows, x2[:]).then_inc(s_out, 16)
                sp.wait_ge(s_out, 16)
            with sp.Else():
                sp.wait_ge(sent, 16 * (NT - C2) * TOPK)

                def load(e, i, g):
                    if g is not None:
                        sp.wait_ge(y_ready, e - RING + 1)
                        sp.dma_start(w_ring[:, i, :], expert_w[bass.ds(e, 1)].rearrange("e p w -> (e p) w")
                                     ).then_inc(w_loaded[i], 16)
                        sp.wait_ge(added[i], 32 * g)
                    elif e < TOPK:
                        sp.wait_ge(last_sent[e], 16 * C2)
                    src = slot_view[bass.ds(e, 1)] if g is not None else slot_view[e:e + 1]
                    sp.dma_start(xs[:, i, :, :], src.rearrange("e p j f -> (e p) j f")).then_inc(xs_loaded[i], 16)

                for i in range(RING):
                    load(i, i, None)
                with sp.Fori(1, E // RING) as g:
                    for i in range(RING):
                        load(g * RING + i, i, g)
                for s in sorted(range(SETS), key=DONE_AT.get):
                    sp.wait_ge(added[DONE_AT[s]], 32 * (E // RING))
                    for q in range(BACK):
                        part = sums[s][q * (T // BACK):(q + 1) * (T // BACK), :].rearrange("(t p) h -> p t h", p=P)
                        sp.dma_start(back[s][:, q * (NT // BACK):(q + 1) * (NT // BACK), :],
                                     part).then_inc(s_back[s][q], 16)
                for q in range(BACK):
                    sp.wait_ge(total_ready, (SETS - 1) * BACK + q + 1)
                    sp.dma_start(out_rows[:, q * (NT // BACK):(q + 1) * (NT // BACK), :],
                                 x2[:, q * (NT // BACK):(q + 1) * (NT // BACK), :]).then_inc(s_out, 16)
                sp.wait_ge(s_out, 16 * BACK)

        @block.tensor
        def _(pe):
            def bank_of(b):
                return ps[:, CONV_BANK[b], :]

            def prep_x(b, c):
                if b == 2 and c == 0:
                    pe.wait_ge(bc_ready, 1)
                    pe.wait_ge(low_ready, 1)
                if b == 3 and c == 0:
                    pe.wait_ge(c_copied, HN // 2)
                if b == 0:
                    pe.wait_ge(conv_w_ready, c + 1)
                if b == 1 and c == 0:
                    pe.wait_ge(s_ctx_rest, 16)
                for k in range(KC):
                    mm = pe.matmul(bank_of(b)[:, c * L:(c + 1) * L], conv_w[:, c, k, :],
                                   ctx_pad[:, b, k:k + L], start=(k == 0), stop=(k == KC - 1))
                mm.then_inc(xc_ready, 1)

            def prep_bc(b):
                pe.wait_ge(u_ready, b + 1)
                if b == 0:
                    pe.wait_ge(s_const, 16 * 3)
                if b == 3:
                    pe.wait_ge(bc_ready, 2)
                    pe.wait_ge(low_ready, 2)
                o = ps[0:104, XDBL_BANK[b], 0:L]
                for c in range(C2):
                    mm = pe.matmul(o, xp_w[:, c, :], u[:, b, c, :], start=(c == 0), stop=(c == C2 - 1))
                mm.then_inc(xdbl_ready, 1)

            def prep_dt(b):
                if b == 0:
                    pe.wait_ge(low_ready, 1)
                elif b == 1:
                    pe.wait_ge(low_ready, 2)
                    pe.wait_ge(c_copied, copies(1, 0))
                else:
                    pe.wait_ge(c_copied, copies(b, 0))
                o = ps[:, DT_BANK[b], :]
                for c in range(C2):
                    mm = pe.matmul(o[:, c * L:(c + 1) * L], dt_w[96:96 + R, c * P:(c + 1) * P],
                                   dt_low[96:96 + R, b, :], start=True, stop=True)
                mm.then_inc(dtv_ready, 1)

            def spread_b(s, q):
                b, c, h = step_of(s)
                pe.wait_ge(bc_ready, b + 1)
                if s >= 1:
                    pe.wait_ge(b_used, 2 * (s - 1) + q + 1)
                for k in range(4):
                    mm = pe.matmul(ps_b[q][:, k * L:(k + 1) * L], sel[:, h * HN + 4 * q + k, :],
                                   bc[:, b, :], start=True, stop=True)
                mm.then_inc(b_ready, 1)

            def spread_c(b, n0, n1):
                for g in range(n0, n1):
                    pe.wait_ge(bc_ready, b + 1)
                    if b == 0:
                        if g == 1:
                            pe.wait_ge(soft_used, 1)
                        if 2 <= g < 5:
                            pe.wait_ge(c_copied, g - 1)
                        if 5 <= g < 7:
                            pe.wait_ge(c_late, g - 4)
                        if g == 7:
                            pe.wait_ge(c_copied, copies(0, 7))
                    elif b >= 1:
                        pe.wait_ge(c_copied, copies(b, max(g - 1, 0)))
                        if g == (0 if b == 1 else 1):
                            pe.wait_ge(soft_used, b + 1)
                        if b == 1 and g == 1:
                            pe.wait_ge(low_ready, 3)
                            pe.wait_ge(bc_ready, 3)
                    for k in range(2):
                        mm = pe.matmul(c_bank(b, g)[:, k * L:(k + 1) * L], sel[:, NS + 2 * g + k, :],
                                       bc[:, b, :], start=True, stop=True)
                    mm.then_inc(c_ready, 1)

            def add_states(s, half):
                b, c, h = step_of(s)
                if half == 0:
                    if s == 0:
                        pe.wait_ge(conv_saved, 1)
                        pe.wait_ge(diag_ready, 1)
                    if c == 0 and h == 0 and b >= 1:
                        pe.wait_ge(yg_ready, b)
                    if h == 0:
                        pe.matmul(ps_y[:, c * L:(c + 1) * L], d_diag[:, c, :], u[:, b, c, :], start=True, stop=False)
                    pe.wait_ge(hc_dve, s + 1)
                mine = HN - POOL_STATES[s]
                if half == 1:
                    pe.wait_ge(hc_pool, s + 1)
                for n in range(mine, HN) if half else range(mine):
                    mm = pe.matmul(ps_y[:, c * L:(c + 1) * L], ident[:], hs[:, s % 2, n, :],
                                   start=False, stop=(h == 1 and n == HN - 1))
                if half == 1:
                    mm.then_inc(y_added, 1)

            def turn_y(b):
                pe.wait_ge(yg_ready, b + 1)
                if b >= 1:
                    pe.wait_ge(rank_used, b)
                else:
                    pe.wait_ge(low_ready, 4)
                    pe.wait_ge(bc_ready, 4)
                for c in range(C2):
                    for lc in range(C2):
                        mm = pe.transpose(ps_post[:, lc * H + c * P:lc * H + (c + 1) * P],
                                          yg[:, c, lc * P:(lc + 1) * P], ident[:])
                mm.then_inc(yT_ready, 1)

            def turn_h(b):
                pe.wait_ge(h_ready, b + 1)
                for lc in range(C2):
                    for c in range(C2):
                        mm = pe.transpose(ps_post[:, c * L + lc * P:c * L + (lc + 1) * P],
                                          rows[:, 2 * b + lc, c * P:(c + 1) * P], ident[:])
                mm.then_inc(hT_psum, 1)

            def router(b):
                pe.wait_ge(hT_ready, b + 1)
                if b == 0:
                    pe.wait_ge(s_router, 16 * 3)
                for lc in range(C2):
                    for c in range(C2):
                        mm = pe.matmul(ps_post[:, lc * E:(lc + 1) * E],
                                       hT[:, c, lc * P:(lc + 1) * P], rt_w[:, c, :],
                                       start=(c == 0), stop=(c == C2 - 1))
                mm.then_inc(logits_ready, 1)

            def ranks(b):
                pe.wait_ge(mask_ready, b + 1)
                strict, ones = tri[:, 0, :], tri[:, 1, :]
                for lc in range(C2):
                    o = ps_post[:, 256 + lc * E:256 + (lc + 1) * E]
                    earlier = [(p, q) for p in range(b) for q in range(C2)] + [(b, q) for q in range(lc)]
                    mm = pe.matmul(o, strict, mask[:, b, lc, :], start=True, stop=not earlier)
                    for p, q in earlier:
                        mm = pe.matmul(o, ones, mask[:, p, q, :], start=False, stop=(p, q) == earlier[-1])
                mm.then_inc(rank_ready, 1)

            pe.wait_ge(s_ctx, 16)
            for c in range(C2):
                prep_x(0, c)
            prep_bc(0)
            prep_dt(0)
            spread_b(0, 0)
            spread_b(0, 1)
            spread_c(0, 0, 1)
            prep_x(1, 0)
            spread_c(0, 1, 2)
            prep_x(1, 1)
            spread_b(1, 0)
            spread_b(1, 1)
            spread_c(0, 2, 4)
            prep_x(2, 0)
            prep_x(2, 1)
            for s in range(STEPS):
                b, c, h = step_of(s)
                k = s % SPB
                groups = C_FIRST if b == 0 else C_GROUPS
                if b >= 1 and k == 1:
                    turn_y(b - 1)
                if s == 1:
                    spread_b(2, 0)
                    spread_b(2, 1)
                    prep_x(3, 0)
                    prep_x(3, 1)
                    spread_c(0, 5, 6)
                if s == 2:
                    prep_dt(1)
                if s >= 1:
                    add_states(s - 1, 0)
                if s == 1:
                    spread_c(0, 6, 7)
                if 3 <= s < STEPS - 1:
                    spread_b(s + 1, 0)
                if b >= 1 and k == 2:
                    turn_h(b - 1)
                if b >= 1 and k == 3:
                    ranks(b - 1)
                if 3 <= s < STEPS - 1:
                    spread_b(s + 1, 1)
                if s >= 1:
                    add_states(s - 1, 1)
                if b >= 1 and k == 2:
                    router(b - 1)
                if s == 0:
                    spread_c(0, 4, 5)
                if s == 1:
                    prep_bc(1)
                    prep_bc(2)
                    spread_b(3, 0)
                    spread_b(3, 1)
                    spread_c(0, 7, 8)
                if s == 2:
                    prep_bc(3)
                if s == 4:
                    spread_c(1, C_FIRST[4], HN)
                if 1 <= b < NB - 1 and k == 0:
                    prep_dt(b + 1)
                if b + 1 < NB:
                    spread_c(b + 1, groups[k], groups[k + 1])
            for half in range(2):
                add_states(STEPS - 1, half)
            turn_y(NB - 1)
            turn_h(NB - 1)
            router(NB - 1)
            ranks(NB - 1)
            pe.wait_ge(rank_used, NB)
            for b in range(NB):
                for q in range(C2):
                    mm = pe.matmul(ps_post[:, 0:E], tri[:, 1, :], mask[:, b, q, :], start=(b + q == 0),
                                   stop=(b == NB - 1 and q == C2 - 1))
            mm.then_inc(count_ready, 1)

            def turn(e, i, g):
                pe.wait_ge(xs_loaded[i], 16 * (g + 1))
                if not (isinstance(e, int) and e < 2):
                    pe.wait_ge(xT_ready, e - 1)
                for j in range(2):
                    for c in range(C2):
                        mm = pe.transpose(ps[:, i % 2, c * CAP + j * HALF:c * CAP + (j + 1) * HALF],
                                          xs[:, i, j, c * P:(c + 1) * P], ident[0:HALF, 0:HALF])
                mm.then_inc(xT_psum, 1)

            def gate_up(e, i, g):
                pe.wait_ge(w_loaded[i], 16 * (g + 1))
                pe.wait_ge(xT_ready, e + 1)
                if not (isinstance(e, int) and e < 2):
                    pe.wait_ge(mid_ready, e - 1)
                for m in range(2):
                    for c in range(C2):
                        w = w_ring[:, i, (m * C2 + c) * I:(m * C2 + c + 1) * I]
                        mm = pe.matmul(ps[:, 2 + i % 2, m * 256:m * 256 + CAP], w, xT[:, i % 2, c, :],
                                       start=(c == 0), stop=(c == C2 - 1))
                mm.then_inc(gu_ready, 1)

            def down(e, i, g):
                pe.wait_ge(split_ready, e + 1)
                if not (isinstance(e, int) and e < 2):
                    pe.wait_ge(y_scaled, e - 1)
                for j in range(2):
                    for n, (a, b) in enumerate(((1, 0), (0, 1), (0, 0))):
                        mm = pe.matmul(ps[0:HALF, 4 + i % 2, j * H:(j + 1) * H],
                                       mid_hl[:, i % 2, a, j * HALF:(j + 1) * HALF], down_hl[:, i % 2, b, :],
                                       start=(n == 0), stop=(n == 2))
                mm.then_inc(y_ready, 1)

            pe.wait_ge(flag_ready, 1)
            overflow = pe.value_load(flag[0:1, 0:1], min_val=0, max_val=1)
            with pe.If(overflow):
                for t in range(NT):
                    if t >= 2:
                        pe.wait_ge(dn_t, t - 1)
                    for c in range(C2):
                        mm = pe.transpose(ps[:, t % 2, c * P:(c + 1) * P], rows[:, t, c * P:(c + 1) * P], ident[:])
                    mm.then_inc(dn_tp, 1)
                pe.wait_ge(dn_t, NT)

                def dense_expert(e, i, g):
                    pe.wait_ge(dn_w[i], 16 * (g + 1))
                    for q in range(2):
                        if not (isinstance(e, int) and e == 0):
                            pe.wait_ge(dn_m, 2 * e + q - 1)
                        for m in range(2):
                            for c in range(C2):
                                w = w_ring[:, i, (m * C2 + c) * I:(m * C2 + c + 1) * I]
                                mm = pe.matmul(ps[:, 2 * q + m, :], w, hT_all[:, c, q * TH:(q + 1) * TH],
                                               start=(c == 0), stop=(c == C2 - 1))
                        mm.then_inc(dn_g, 1)
                    for q in range(2):
                        pe.wait_ge(dn_m, 2 * e + q + 1)
                        if not (isinstance(e, int) and e == 0):
                            pe.wait_ge(dn_acc, 2 * e + q - 1)
                        for t in range(NT // 2):
                            mm = pe.matmul(ps[:, 4 + 2 * q + t // 2, t % 2 * H:(t % 2 + 1) * H],
                                           mid_all[:, q, t * P:(t + 1) * P], w_ring[:, i, 2 * C2 * I:WROW],
                                           start=True, stop=True)
                        mm.then_inc(dn_y, 1)

                for i in range(2):
                    dense_expert(i, i, 0)
                with pe.Fori(1, E // 2) as g:
                    for i in range(2):
                        dense_expert(2 * g + i, i, g)
            with pe.Else():
                for e in range(RING):
                    turn(e, e, 0)
                    if e >= 1:
                        gate_up(e - 1, e - 1, 0)
                    if e >= 2:
                        down(e - 2, e - 2, 0)
                with pe.Fori(1, E // RING) as g:
                    for i in range(RING):
                        e = g * RING + i
                        turn(e, i, g)
                        gate_up(e - 1, (i - 1) % RING, g if i >= 1 else g - 1)
                        down(e - 2, (i - 2) % RING, g if i >= 2 else g - 1)
                gate_up(E - 1, RING - 1, E // RING - 1)
                down(E - 2, RING - 2, E // RING - 1)
                down(E - 1, RING - 1, E // RING - 1)

        @block.scalar
        def _(act):
            def copy_c(b, n0, n1):
                for g in range(n0, n1):
                    if g == 0 and b >= 2:
                        act.wait_ge(hc_pool, SPB * (b - 1))
                        act.wait_ge(hc_dve, SPB * (b - 1))
                    act.wait_ge(c_ready, b * HN + g + 1)
                    act.activation(c_sb[:, b % 2, 2 * g:2 * g + 2, :].rearrange("p n l -> p (n l)"),
                                   c_bank(b, g), ACT.Copy).then_inc(c_copied, 1)

            def silu_u(b):
                if b == 3:
                    act.wait_ge(conv_saved, 1)
                    act.activation(u[:, b], u[:, b], ACT.Silu).then_inc(u_ready, 1)
                    return
                act.wait_ge(xc_ready, C2 * (b + 1))
                for c in range(C2):
                    last = act.activation(u[:, b, c, :], ps[:, CONV_BANK[b], c * L:(c + 1) * L], ACT.Silu,
                                          bias=vecs[:, c, CB:CB + 1])
                last.then_inc(u_ready, 1)

            def silu_z(b):
                if b == 0:
                    act.wait_ge(z_stats, 1)
                for c in range(C2):
                    t = 2 * b + c
                    last = act.activation(gz[:, b, c, :], x_sb[:, t, :], ACT.Silu, bias=nmr[:, t, :],
                                          scale=rstd[:, t, :])
                last.then_inc(gz_ready, 1)

            def prep_low(b):
                act.wait_ge(xdbl_ready, b + 1)
                act.activation(dt_low[96:96 + R, b, :], ps[96:96 + R, XDBL_BANK[b], 0:L],
                               ACT.Copy).then_inc(low_ready, 1)

            def prep_soft(b):
                act.wait_ge(dtv_ready, b + 1)
                if b >= 1:
                    act.wait_ge(dt_ready, 2 * b)
                src = ps[:, DT_BANK[b], :]
                for c in range(C2):
                    last = act.activation(dt_abs[:, c, :], src[:, c * L:(c + 1) * L], ACT.Abs,
                                          bias=vecs[:, c, DTB:DTB + 1])
                last.then_inc(act_soft, 1)
                for c in range(C2):
                    last = act.activation(dt_pos[:, c, :], src[:, c * L:(c + 1) * L], ACT.Relu,
                                          bias=vecs[:, c, DTB:DTB + 1])
                last.then_inc(soft_used, 1)
                act.wait_ge(act_soft, 2 * b + 1)
                act.activation(dt_e[:], dt_abs[:], ACT.Exp, scale=-1.0).then_inc(act_soft, 1)
                act.wait_ge(act_soft, 2 * b + 2)
                act.activation(dt_ln[:], dt_e[:], ACT.Ln, bias=1.0).then_inc(soft_ready, 1)

            def decay(s, n0=0, n1=HN):
                b, c, h = step_of(s)
                act.wait_ge(dt_ready, 2 * b + 1)
                if s == 0:
                    act.wait_ge(edges, 1)
                    act.wait_ge(a_ready, 1)
                if s >= 2:
                    act.wait_ge(scan_done, s - 1)
                for n in range(n0, n1):
                    last = act.activation(dA[:, s % 2, n, 1:L], dt[:, b % 2, c, 1:L], ACT.Exp,
                                          scale=a_neg[:, c, h * HN + n:h * HN + n + 1])
                if n1 == HN:
                    last.then_inc(dA_ready, 1)

            def root(var, rstd, ready, done, b):
                act.wait_ge(ready, b + 1)
                act.activation(rstd[:], var[:], ACT.Ln).then_inc(done, 1)
                act.wait_ge(done, 2 * b + 1)
                act.activation(rstd[:], rstd[:], ACT.Exp, scale=-0.5).then_inc(done, 1)

            def norm_h(b):
                act.wait_ge(x2_stats, b + 1)
                for lc in range(C2):
                    last = act.activation(rows[:, 2 * b + lc, 0:H], x2[:, 2 * b + lc, :], ACT.Identity,
                                          bias=nmr2[:, lc, :], scale=rstd2[:, lc, :])
                last.then_inc(h_ready, 1)

            def copy_hT(b):
                act.wait_ge(hT_psum, b + 1)
                act.activation(hT[:], ps_post.rearrange("p (c l) -> p c l", c=C2),
                               ACT.Copy).then_inc(hT_ready, 1)

            def exp_router(b):
                act.wait_ge(max_ready, b + 1)
                for lc in range(C2):
                    last = act.activation(ex[:, lc, :], ps_post[:, lc * E:(lc + 1) * E], ACT.Exp,
                                          bias=neg_max[:, lc:lc + 1], accum_out=ex_sum[:, lc:lc + 1])
                last.then_inc(ex_ready, 1)

            act.preload_act_table_set("silu_and_others")
            act.wait_ge(s_small, 16)
            silu_u(0)
            prep_low(0)
            act.preload_act_table_set("natural_log_exp_and_others")
            act.activation(a_exp[:], vecs[:, :, AL:AL + NS], ACT.Exp).then_inc(act_seq, 1)
            act.wait_ge(act_seq, 1)
            act.activation(a_neg[:], a_exp[:], ACT.Copy, scale=-1.0).then_inc(a_ready, 1)
            prep_soft(0)
            root(var, rstd, z_var, z_root, 0)
            copy_c(0, 0, 1)
            decay(0)
            copy_c(0, 1, 3)
            decay(1)
            copy_c(0, 3, 4)
            decay(2)
            decay(3)
            act.preload_act_table_set("silu_and_others")
            silu_u(1)
            silu_u(2)
            silu_z(0)
            copy_c(0, 6, 7)
            silu_z(1)
            prep_low(1)
            copy_c(0, 7, 8)
            prep_low(2)
            silu_z(2)
            silu_z(3)
            silu_u(3)
            act.preload_act_table_set("natural_log_exp_and_others")
            for s in range(2, STEPS):
                b, c, h = step_of(s)
                k = s % SPB
                groups = C_FIRST if b == 0 else C_GROUPS
                if b >= 1 and k == 2:
                    norm_h(b - 1)
                if s == 2:
                    prep_soft(1)
                if 3 <= s < STEPS - 1:
                    decay(s + 1, 0, HN // 2)
                if b >= 1 and k == 2:
                    copy_hT(b - 1)
                if 3 <= s < STEPS - 1:
                    decay(s + 1, HN // 2, HN)
                if b >= 1 and k == 2:
                    exp_router(b - 1)
                if b >= 1 and k == 1:
                    root(var2, rstd2, x2_var, x2_root, b - 1)
                if s == 3:
                    prep_low(3)
                if s == 4:
                    copy_c(1, C_FIRST[4], HN)
                if 1 <= b < NB - 1 and k == 0:
                    prep_soft(b + 1)
                if b + 1 < NB:
                    copy_c(b + 1, groups[k], groups[k + 1])
            root(var2, rstd2, x2_var, x2_root, NB - 1)
            norm_h(NB - 1)
            copy_hT(NB - 1)
            exp_router(NB - 1)

            def silu_gate(e, i, g):
                act.wait_ge(gu_ready, e + 1)
                if not (isinstance(e, int) and e < 2):
                    act.wait_ge(mid_ready, e - 1)
                act.activation(sg[:, i % 2, :], ps[:, 2 + i % 2, 0:CAP], ACT.Silu).then_inc(sg_ready, 1)

            def scale_y(e, i, g):
                act.wait_ge(y_ready, e + 1)
                act.wait_ge(ws_ready, e + 1)
                if not (isinstance(g, int) and g == 0):
                    act.wait_ge(added[i], 32 * g)
                for j in range(2):
                    last = act.activation(y_sb[:, i, j, :], ps[0:HALF, 4 + i % 2, j * H:(j + 1) * H],
                                          ACT.Copy, scale=w_slot[:, i, j:j + 1])
                last.then_inc(y_scaled, 1)

            act.wait_ge(flag_ready, 1)
            overflow = act.value_load(flag[0:1, 0:1], min_val=0, max_val=1)
            with act.If(overflow):
                def dense_silu(e):
                    for q in range(2):
                        act.wait_ge(dn_g, 2 * e + q + 1)
                        if not (isinstance(e, int) and e == 0):
                            act.wait_ge(dn_m, 2 * e + q - 1)
                        act.activation(sg_all[:, q, :], ps[:, 2 * q, :], ACT.Silu).then_inc(dn_s, 1)

                dense_silu(0)
                with act.Fori(1, E) as e:
                    dense_silu(e)
            with act.Else():
                for e in range(RING):
                    silu_gate(e, e, 0)
                    if e >= 1:
                        scale_y(e - 1, e - 1, 0)
                with act.Fori(1, E // RING) as g:
                    for i in range(RING):
                        e = g * RING + i
                        silu_gate(e, i, g)
                        scale_y(e - 1, (i - 1) % RING, g if i >= 1 else g - 1)
                scale_y(E - 1, RING - 1, E // RING - 1)

        @block.gpsimd
        def _(pool):
            pool.iota(fill[:, :, ROW - 1].bitcast(U32), [[1, 2]], base=SPARE, channel_multiplier=2).then_inc(fill_made, 1)
            pool.iota(rows[:, :, ROW - 1].bitcast(U32), [[P, NT]], base=0, channel_multiplier=1).then_inc(id_made, 1)

            def soft(b, half):
                mine = b - DVE_SOFT
                if half == 0:
                    pool.wait_ge(soft_ready, b + 1)
                    pool.wait_ge(e1_ready, mine + 1)
                    pool.tensor_tensor(dt_t[:], dt_e[:], dt_t[:], ALU.subtract).then_inc(pool_seq, 1)
                    pool.wait_ge(pool_seq, 2 * mine + 1)
                    pool.tensor_tensor(dt_t[:], dt_ln[:], dt_t[:], ALU.add).then_inc(pool_seq, 1)
                else:
                    pool.wait_ge(pool_seq, 2 * mine + 2)
                    pool.wait_ge(scan_done, SPB * (b - 1))
                    pool.tensor_tensor(dt[:, b % 2], dt_pos[:], dt_t[:], ALU.add).then_inc(dt_ready, 1)
                    pool.wait_ge(dt_ready, 2 * b + 1)
                    pool.tensor_tensor(du[:, b % 2], dt[:, b % 2], u[:, b], ALU.mult).then_inc(dt_ready, 1)

            def times_c(s):
                b, c, h = step_of(s)
                pool.wait_ge(scan_done, s + 1)
                if b == 0 and h == 1:
                    pool.wait_ge(c_late, 2)
                pool.wait_ge(c_copied, copies(b, h * HN // 2 + HN // 2))
                n = POOL_STATES[s]
                a = hs[:, s % 2, HN - n:HN, :]
                pool.tensor_tensor(a, a, c_sb[:, b % 2, (h + 1) * HN - n:(h + 1) * HN, :],
                                   ALU.mult).then_inc(hc_pool, 1)

            def send(b, lo, hi):
                if lo == 0:
                    pool.wait_ge(place_ready, b + 1)
                    pool.wait_ge(weights_ready, b + 1)
                    if b == 0:
                        pool.wait_ge(fill_done, 16 * (4 + SETS))
                        pool.wait_ge(id_made, 1)
                for k in range(lo, hi):
                    t = 2 * b + k // TOPK
                    pool.indirect_dma_start(
                        slots, bass.IndirectOffsetOnAxis(slot_of[:, t, k % TOPK:k % TOPK + 1], 0),
                        rows[:, t, :], None).then_inc(sent, 16)

            pool.memset(tick[:], 0.0).then_inc(ticked, 1)
            for s in range(STEPS):
                b, c, h = step_of(s)
                k = s % SPB
                times_c(s)
                if k in (1, 2) and DVE_SOFT <= b + 1 < NB:
                    soft(b + 1, k - 1)
                if k == 3 and b >= 1:
                    send(b - 1, 0, SENDS[0])
                if k < 3 and b >= 2:
                    send(b - 2, SENDS[k], SENDS[k + 1])
            send(NB - 2, SENDS[0], 2 * TOPK)

            def send_last():
                pool.wait_ge(place_ready, NB)
                pool.wait_ge(weights_ready, NB)
                for k in range(TOPK):
                    for t in range(NT - C2, NT):
                        pool.indirect_dma_start(
                            slots, bass.IndirectOffsetOnAxis(slot_of[:, t, k:k + 1], 0),
                            rows[:, t, :], None).then_inc(last_sent[k], 16)

            def add_rows(e, i, g):
                pool.wait_ge(y_scaled, e + 1)
                sets = SET_LAST if isinstance(g, int) and g else SET_OF
                earlier = [(j, g) for j in range(i) if sets[j] == sets[i]]
                if not isinstance(g, int) or g:
                    earlier = [(j, g - 1) for j in range(RING) if SET_OF[j] == sets[i]] + earlier
                if earlier:
                    place, ring = earlier[-1]
                    pool.wait_ge(added[place], 32 * (ring + 1))
                if not isinstance(g, int):
                    pool.wait_ge(ticked, e - RING + 1)
                    pool.tensor_tensor(tick[:, 1:2], tick[:, 0:1], tick[:, 0:1], ALU.add).then_inc(ticked, 1)
                for j in range(2):
                    pool.indirect_dma_start(
                        sums[sets[i]], bass.IndirectOffsetOnAxis(xs[:, i, j, ROW - 1:ROW].bitcast(U32), 0),
                        y_sb[:, i, j, :], None, compute_op=ALU.add).then_inc(added[i], 16)

            send_last()
            pool.wait_ge(flag_ready, 1)
            overflow = pool.value_load(flag[0:1, 0:1], min_val=0, max_val=1)
            with pool.If(overflow):
                pool.wait_ge(sent, 16 * (NT - C2) * TOPK)
                for k in range(TOPK):
                    pool.wait_ge(last_sent[k], 16 * C2)
            with pool.Else():
                for e in range(RING):
                    add_rows(e, e, 0)
                with pool.Fori(1, E // RING - 1) as g:
                    for i in range(RING):
                        add_rows(g * RING + i, i, g)
                for i in range(RING):
                    add_rows(E - RING + i, i, E // RING - 1)

        @block.vector
        def _(dve):
            seq = [0]

            def link(ins):
                ins.then_inc(dve_seq, 1)
                seq[0] += 1
                dve.wait_ge(dve_seq, seq[0])

            def one_plus(b):
                dve.wait_ge(act_soft, 2 * b + 2)
                if b >= 1:
                    dve.wait_ge(dt_ready, 2 * b)
                return dve.tensor_scalar(dt_t[:], dt_e[:], 1.0, -1.0, ALU.add, ALU.add)

            def soft(b):
                link(one_plus(b))
                link(dve.tensor_tensor(dt_t[:], dt_e[:], dt_t[:], ALU.subtract))
                dve.wait_ge(soft_ready, b + 1)
                link(dve.tensor_tensor(dt_t[:], dt_ln[:], dt_t[:], ALU.add))
                dve.tensor_tensor(dt[:, b], dt_pos[:], dt_t[:], ALU.add).then_inc(dt_ready, 1)
                dve.wait_ge(dt_ready, 2 * b + 1)
                dve.tensor_tensor(du[:, b], dt[:, b], u[:, b], ALU.mult).then_inc(dt_ready, 1)

            def prep_parts(b):
                dve.wait_ge(xdbl_ready, b + 1)
                s = bc[:, b, :]
                src = ps[0:96, XDBL_BANK[b], 0:L]
                link(dve.tensor_copy(s, src))
                link(dve.tensor_tensor(bc_rest[:], src, s, ALU.subtract))
                dve.tensor_copy(s[32:64], bc_rest[32:64])
                link(dve.tensor_copy(s[64:96], bc_rest[64:96]))
                dve.tensor_tensor(s[64:96], bc_rest[64:96], s[64:96], ALU.subtract).then_inc(bc_ready, 1)

            def stats(src, st, mv, var):
                for c in range(src.shape[1]):
                    ins = dve.bn_stats(st[:, c, :], src[:, c, :])
                link(ins)
                for c in range(src.shape[1]):
                    ins = dve.bn_aggr(mv[:, c, :], st[:, c, :])
                link(ins)
                return dve.tensor_scalar(var[:], mv[:, :, 1:2], LN_EPS, None, ALU.add)

            def scales(mv, var, rstd, newton, nmr):
                link(dve.tensor_tensor(newton[:], rstd[:], rstd[:], ALU.mult))
                link(dve.tensor_tensor(newton[:], newton[:], var[:], ALU.mult))
                link(dve.tensor_scalar(newton[:], newton[:], -0.5, 1.5, ALU.mult, ALU.add))
                link(dve.tensor_tensor(rstd[:], rstd[:], newton[:], ALU.mult))
                return dve.scalar_tensor_tensor(nmr[:], mv[:, :, 0:1], -1.0, rstd[:], ALU.mult, ALU.mult)

            def step_inputs(s, q0=0, q1=2):
                b, c, h = step_of(s)
                dve.wait_ge(dt_ready, 2 * b + 2)
                if s >= 1:
                    dve.wait_ge(scan_done, s)
                for q in range(q0, q1):
                    dve.wait_ge(b_ready, 2 * s + q + 1)
                    ins = dve.tensor_tensor(
                        dBu[:, 4 * q:4 * q + 4, :], ps_b[q].rearrange("p (n l) -> p n l", n=4),
                        du[:, b % 2, c, :].unsqueeze(1).to_broadcast([P, 4, L]), ALU.mult)
                    ins.then_inc(b_used, 1)

            def scan_step(s):
                dve.wait_ge(b_used, 2 * s + 2)
                dve.wait_ge(dA_ready, s + 1)
                if s >= 2:
                    dve.wait_ge(y_added, s - 1)
                dve.tensor_tensor_scan(
                    hs[:, s % 2].rearrange("p n l -> p (n l)"), dA[:, s % 2].rearrange("p n l -> p (n l)"),
                    dBu[:].rearrange("p n l -> p (n l)"), 0.0, ALU.mult, ALU.add).then_inc(scan_done, 1)

            def copy_c(g):
                dve.wait_ge(c_ready, g + 1)
                dve.tensor_copy(c_sb[:, 0, 2 * g:2 * g + 2, :].rearrange("p n l -> p (n l)"),
                                c_bank(0, g)).then_inc(c_late, 1)

            def save_conv():
                dve.wait_ge(xc_ready, C2 * NB)
                for c in range(C2):
                    ins = dve.tensor_scalar(u[:, 3, c, :], ps[:, CONV_BANK[3], c * L:(c + 1) * L],
                                            vecs[:, c, CB:CB + 1], None, ALU.add)
                ins.then_inc(conv_saved, 1)

            def times_c(s):
                b, c, h = step_of(s)
                dve.wait_ge(scan_done, s + 1)
                if b == 0 and h == 1:
                    dve.wait_ge(c_late, 2)
                dve.wait_ge(c_copied, copies(b, h * HN // 2 + HN // 2))
                n = POOL_STATES[s]
                a = hs[:, s % 2, 0:HN - n, :]
                dve.tensor_tensor(a, a, c_sb[:, b % 2, h * HN:(h + 1) * HN - n, :],
                                  ALU.mult).then_inc(hc_dve, 1)

            def gated(b):
                dve.wait_ge(y_added, SPB * (b + 1))
                dve.wait_ge(gz_ready, b + 1)
                dve.tensor_tensor(yg[:], ps_y.rearrange("p (c l) -> p c l", c=C2), gz[:, b],
                                  ALU.mult).then_inc(yg_ready, 1)

            def residual(b):
                dve.wait_ge(yT_ready, b + 1)
                tiles = x2[:, 2 * b:2 * b + 2, :]
                link(dve.tensor_tensor(tiles, ps_post.rearrange("p (t h) -> p t h", h=H),
                                       x_sb[:, 2 * b:2 * b + 2, :], ALU.add))
                if b >= 1:
                    dve.wait_ge(h_ready, b)
                stats(tiles, st2, mv2, var2).then_inc(x2_var, 1)

            def x2_scales(b):
                dve.wait_ge(x2_root, 2 * b + 2)
                scales(mv2, var2, rstd2, newton2, nmr2).then_inc(x2_stats, 1)

            def router_max(b):
                dve.wait_ge(logits_ready, b + 1)
                if b >= 1:
                    dve.wait_ge(ex_ready, b)
                dve.tensor_reduce(neg_max[:], ps_post[:, 0:C2 * E].rearrange("p (t e) -> p t e", e=E), AX_X,
                                  ALU.max, negate=True).then_inc(max_ready, 1)

            def choose(b):
                dve.wait_ge(ex_ready, b + 1)
                for t in range(C2):
                    ins = dve.max(top[:, t, :], ex[:, t, :])
                link(ins)
                for t in range(C2):
                    ins = dve.match_replace(rest[:, t, :], top[:, t, :], ex[:, t, :], -1.0)
                link(ins)
                dve.tensor_scalar(mask[:, b], rest[:], 0.0, None, ALU.is_lt).then_inc(mask_ready, 1)

            def weights(b):
                link(dve.reciprocal(inv_sum[:], ex_sum[:]))
                dve.wait_ge(mask_ready, b + 1)
                for t in range(C2):
                    ins = dve.scalar_tensor_tensor(rows[:, 2 * b + t, H:H + E], ex[:, t, :], inv_sum[:, t:t + 1],
                                                   mask[:, b, t, :], ALU.mult, ALU.mult)
                ins.then_inc(weights_ready, 1)

            def places(b):
                dve.wait_ge(rank_ready, b + 1)
                rank = ps_post[:, 256:256 + C2 * E]
                dve.scalar_tensor_tensor(r_over[:], rank, float(CAP), place[:, 0, :], ALU.is_ge, ALU.mult)
                dve.scalar_tensor_tensor(r_key[:], rank, -1.0, place[:, 1, :], ALU.mult,
                                         ALU.add).then_inc(rank_used, 1)
                dve.wait_ge(rank_used, b + 1)
                link(dve.tensor_tensor(r_key[:], r_key[:], r_over[:], ALU.subtract))
                link(dve.tensor_tensor(r_key[:], r_key[:], mask[:, b].rearrange("p t e -> p (t e)"), ALU.mult))
                for t in range(C2):
                    ins = dve.max(key_top[:, t, :], r_key[:, t * E:(t + 1) * E])
                link(ins)
                dve.tensor_scalar(slot_of[:, 2 * b:2 * b + 2, :], key_top[:], -1.0, float(KEY), ALU.mult,
                                  ALU.add).then_inc(place_ready, 1)

            dve.memset(fill[:, :, 0:ROW - 1], 0.0).then_inc(fill_made, 1)
            dve.memset(dA[:, :, :, 0:1], 0.0).then_inc(edges, 1)
            dve.wait_ge(s_taps, 32)
            for c in range(C2):
                part = slice(c * P, (c + 1) * P)
                dve.tensor_tensor(conv_w[:, c], taps[:, :, part],
                                  in_proj[:, part].unsqueeze(1).to_broadcast([P, KC, P]),
                                  ALU.mult).then_inc(conv_w_ready, 1)
            dve.wait_ge(s_small, 16)
            dve.wait_ge(s_x, 16)
            stats(x_sb[:], st, mv, var).then_inc(z_var, 1)
            dve.wait_ge(s_ident, 16)
            for c in range(C2):
                ins = dve.tensor_scalar(d_diag[:, c, :], ident[:], vecs[:, c, DD:DD + 1], None, ALU.mult)
            ins.then_inc(diag_ready, 1)
            prep_parts(0)
            soft(0)
            for s in range(STEPS):
                b, c, h = step_of(s)
                k = s % SPB
                step_inputs(s, 0, 1)
                if s == 2:
                    copy_c(5)
                if b >= 1 and k == 3:
                    choose(b - 1)
                step_inputs(s, 1, 2)
                if b >= 1 and k == 1:
                    residual(b - 1)
                if b >= 1 and k == 3:
                    weights(b - 1)
                    places(b - 1)
                if s == 3:
                    soft(1)
                if k == 1 and DVE_SOFT <= b + 1 < NB:
                    one_plus(b + 1).then_inc(e1_ready, 1)
                scan_step(s)
                if s == 0:
                    dve.wait_ge(z_root, 2)
                    scales(mv, var, rstd, newton, nmr).then_inc(z_stats, 1)
                if s == 1:
                    times_c(0)
                    copy_c(4)
                    save_conv()
                if s == 2:
                    times_c(1)
                if s >= 2:
                    times_c(s)
                if s == 2:
                    prep_parts(1)
                if s == 3:
                    prep_parts(2)
                if s == 4:
                    prep_parts(3)
                if b >= 1 and k == 0:
                    gated(b - 1)
                if b >= 1 and k == 1:
                    x2_scales(b - 1)
                if b >= 1 and k == 2:
                    router_max(b - 1)
            gated(NB - 1)
            residual(NB - 1)
            x2_scales(NB - 1)
            router_max(NB - 1)
            choose(NB - 1)
            weights(NB - 1)
            places(NB - 1)
            dve.wait_ge(count_ready, 1)
            link(dve.tensor_reduce(count[:], ps_post[:, 0:E], AX_X, ALU.max))
            dve.tensor_scalar(flag[:], count[:], float(CAP), None, ALU.is_gt).then_inc(flag_ready, 1)

            def copy_rows(e, i, g):
                dve.wait_ge(xT_psum, e + 1)
                if not (isinstance(e, int) and e < 2):
                    dve.wait_ge(gu_ready, e - 1)
                dve.tensor_copy(xT[:, i % 2], ps[:, i % 2, 0:C2 * CAP].rearrange("p (c s) -> p c s", c=C2)
                                ).then_inc(xT_ready, 1)
                col = xs[:, i, :, bass.ds(H + e, 1)].rearrange("p j o -> p (j o)")
                if not (isinstance(g, int) and g == 0):
                    dve.wait_ge(y_scaled, e - RING + 1)
                dve.tensor_copy(w_slot[:, i, :], col).then_inc(ws_ready, 1)

            def middle(e, i, g):
                dve.wait_ge(sg_ready, e + 1)
                if not (isinstance(e, int) and e < 2):
                    dve.wait_ge(y_ready, e - 1)
                m, w = mid[:, i % 2, :], w_ring[:, i, 2 * C2 * I:WROW]
                dve.tensor_tensor(m, sg[:, i % 2, :], ps[:, 2 + i % 2, 256:256 + CAP],
                                  ALU.mult).then_inc(mid_ready, 1)
                dve.tensor_copy(down_hl[:, i % 2, 0, :], w)
                dve.wait_ge(mid_ready, e + 1)
                dve.tensor_copy(mid_hl[:, i % 2, 0, :], m).then_inc(high_ready, 1)
                dve.wait_ge(high_ready, e + 1)
                dve.tensor_tensor(down_hl[:, i % 2, 1, :], w, down_hl[:, i % 2, 0, :].bitcast(F32), ALU.subtract)
                dve.tensor_tensor(mid_hl[:, i % 2, 1, :], m, mid_hl[:, i % 2, 0, :].bitcast(F32), ALU.subtract
                                  ).then_inc(split_ready, 1)

            dve.wait_ge(flag_ready, 1)
            overflow = dve.value_load(flag[0:1, 0:1], min_val=0, max_val=1)
            with dve.If(overflow):
                for t in range(NT):
                    dve.wait_ge(dn_tp, t + 1)
                    dve.tensor_copy(hT_all[:, :, t * P:(t + 1) * P],
                                    ps[:, t % 2, 0:C2 * P].rearrange("p (c m) -> p c m", c=C2)).then_inc(dn_t, 1)

                def dense_sums(e, i):
                    if not isinstance(e, int):
                        dve.wait_ge(dn_acc, 2 * e - 2)
                    dve.tensor_copy(w_tok[:, i, :], rows[:, :, bass.ds(H + e, 1)].rearrange("p t o -> p (t o)")
                                    ).then_inc(dn_wt, 1)
                    for q in range(2):
                        dve.wait_ge(dn_s, 2 * e + q + 1)
                        if not (isinstance(e, int) and e == 0):
                            dve.wait_ge(dn_y, 2 * e + q - 1)
                        dve.tensor_tensor(mid_all[:, q, :], sg_all[:, q, :], ps[:, 2 * q + 1, :],
                                          ALU.mult).then_inc(dn_m, 1)
                    dve.wait_ge(dn_wt, e + 1)
                    for q in range(2):
                        dve.wait_ge(dn_y, 2 * e + q + 1)
                        if not (isinstance(e, int) and e == 0):
                            dve.wait_ge(dn_acc, 2 * e + q - 1)
                        for t in range(NT // 2):
                            tile = x2[:, q * NT // 2 + t, :]
                            k = q * NT // 2 + t
                            ins = dve.scalar_tensor_tensor(
                                tile, ps[:, 4 + 2 * q + t // 2, t % 2 * H:(t % 2 + 1) * H], w_tok[:, i, k:k + 1],
                                tile, ALU.mult, ALU.add)
                        ins.then_inc(dn_acc, 1)

                for i in range(2):
                    dense_sums(i, i)
                with dve.Fori(1, E // 2) as g:
                    for i in range(2):
                        dense_sums(2 * g + i, i)
            with dve.Else():
                for e in range(RING):
                    copy_rows(e, e, 0)
                    if e >= 1:
                        middle(e - 1, e - 1, 0)
                with dve.Fori(1, E // RING) as g:
                    for i in range(RING):
                        e = g * RING + i
                        copy_rows(e, i, g)
                        middle(e - 1, (i - 1) % RING, g if i >= 1 else g - 1)
                middle(E - 1, RING - 1, E // RING - 1)
                for n, s in enumerate(sorted(range(SETS), key=DONE_AT.get)):
                    for q in range(BACK):
                        dve.wait_ge(s_back[s][q], 16)
                        if n:
                            dve.wait_ge(total_ready, (n - 1) * BACK + q + 1)
                        part = slice(q * (NT // BACK), (q + 1) * (NT // BACK))
                        dve.tensor_tensor(x2[:, part, :], x2[:, part, :], back[s][:, part, :],
                                          ALU.add).then_inc(total_ready, 1)



def layout(inputs):
    a = {k: np.ascontiguousarray(v) for k, v in inputs.items()}
    chunks = lambda w: np.ascontiguousarray(w.reshape(C2, P, -1).transpose(1, 0, 2))
    ctxT = a["ctx_1024"].transpose(2, 0, 1)
    ctxT = np.concatenate([np.zeros((DM, NB, KC - 1), np.float32), ctxT], 2)
    xp = a["L0_xattn_x_proj_w"].T
    bc = xp[:, R:]
    gate, up, down = (a[f"L0_ffn_w_{n}"] for n in ("gate", "up", "down"))
    turned = lambda w: w.transpose(0, 2, 1).reshape(E, C2, P, I).transpose(0, 2, 1, 3).reshape(E, P, C2 * I)
    d = {
        "x": a["x"],
        "ctxT": ctxT,
        "in_projT": a["L0_xattn_in_proj_w"].T,
        "taps": a["L0_xattn_conv_w"].reshape(DI, KC).T[None],
        "vecs": chunks(np.concatenate([
            a["L0_xattn_conv_b"][:, None], a["L0_xattn_dt_proj_b"][:, None],
            a["L0_xattn_D"][:, None], a["L0_xattn_A_log"]], 1)),
        "xp_w": chunks(np.concatenate([bc, bc, bc, xp[:, :R]], 1)),
        "dt_wT": a["L0_xattn_dt_proj_w"].T,
        "rt_w": chunks(a["L0_ffn_router_w"].T),
        "w_all": np.concatenate([turned(gate), turned(up), down.transpose(0, 2, 1)], 2),
    }
    d.update(consts())
    return {k: np.ascontiguousarray(v) for k, v in d.items()}


def kernel(**inputs):
    import concourse.bacc as _bacc
    from concourse.bass_utils import run_bass_kernel_spmd as _run

    nc = _bacc.Bacc("TRN2", target_bir_lowering=False, num_devices=1)
    arrays, aps = {}, {}
    for name, v in layout(inputs).items():
        arrays[f"in_{name}"] = v
        aps[name] = nc.dram_tensor(f"in_{name}", v.shape, mybir.dt.from_np(v.dtype), kind="ExternalInput").ap()
    out = nc.dram_tensor("out_0", (NB, L, H), F32, kind="ExternalOutput").ap()
    program(nc, aps, out)
    r = _run(nc, [arrays], core_ids=[0])
    return r.results[0]["out_0"]
```
